# Optimizing a Trainium2 kernel written in Bass

```python
import numpy as np
import jax
import jax.numpy as jnp

def _softmax(x, axis=-1):
    return jax.nn.softmax(x, axis=axis)

def _gelu(x):
    return jax.nn.gelu(x, approximate=True)

def _silu(x):
    return jax.nn.silu(x)

def _sigmoid(x):
    return jax.nn.sigmoid(x)

def _layernorm(x, axis=-1, eps=1e-05):
    m = jnp.mean(x, axis=axis, keepdims=True)
    v = jnp.var(x, axis=axis, keepdims=True)
    return (x - m) / jnp.sqrt(v + eps)

def _scatter_add(tgt, idx, src, axis=0):
    return tgt.at[idx].add(src)

def _segment_sum(src, seg, n):
    return jax.ops.segment_sum(src, seg, n)
kernel_name = 'mk_cond_resid_d2_seqx_r4_4d42ba'

def setup_inputs(seed: int=0):
    np.random.seed(seed)
    _w = jnp.asarray

    def _rec_inputs():
        import jax
        import jax.numpy as jnp
        _rk = jax.random.key(seed)
        x = -0.0003929 + 0.9999 * jax.random.normal(jax.random.fold_in(_rk, 1), (32, 256, 256), jnp.float32)
        _lenS = 256 - jax.random.randint(jax.random.fold_in(_rk, 7), (32,), 0, max(1, 256 // 4) + 1, jnp.int32)
        _lenS2 = 256 - jax.random.randint(jax.random.fold_in(_rk, 8), (32,), 0, max(1, 256 // 4) + 1, jnp.int32)
        cond_1024 = 0.00386106 + 1.00199 * jax.random.normal(jax.random.fold_in(_rk, 11), (32, 256), jnp.float32)
        return (x, cond_1024)
    x, cond_1024 = _rec_inputs()

    def _L0_cond_setup():
        import jax, jax.numpy as jnp
        import numpy as np
        RANK = 8
        LN_EPS = 1e-05
        key = jax.random.key(seed)
        ks = jax.random.split(key, 8)
        B, T, D = (16, 256, 256)
        A = 256
        I = 256
        OUT = D * RANK * 4
        s = 0.02
        return {'x': jax.random.normal(ks[0], (B, T, D), jnp.float32), 'ada_emb': jax.random.normal(ks[1], (B, A), jnp.float32), 'base_up': jax.random.normal(ks[2], (D, D), jnp.float32) * s, 'base_down': jax.random.normal(ks[3], (D, D), jnp.float32) * s, 'ln_gamma': jnp.ones((A,), jnp.float32), 'ln_beta': jnp.zeros((A,), jnp.float32), 'W1': jax.random.normal(ks[4], (A, I), jnp.float32) / np.sqrt(A), 'bias1': jnp.zeros((I,), jnp.float32), 'W2': jax.random.normal(ks[5], (I, OUT), jnp.float32) / np.sqrt(I), 'bias2': jnp.zeros((OUT,), jnp.float32)}
    _L0_cond_all = _L0_cond_setup()
    _L0_cond_in = {k: v for k, v in _L0_cond_all.items() if k in ('base_up', 'base_down', 'ln_gamma', 'ln_beta', 'W1', 'bias1', 'W2', 'bias2')}
    del _L0_cond_all

    def _L1_cond_setup():
        import jax, jax.numpy as jnp
        import numpy as np
        LATENT = 256
        key = jax.random.key(seed)
        k1, k2, k3, k4 = jax.random.split(key, 4)
        B, T, D = (64, 128, LATENT)
        h_t = jax.random.normal(k1, (B, D), dtype=jnp.float32)
        z = jax.random.normal(k2, (B, T, D), dtype=jnp.float32)
        bound = 1.0 / np.sqrt(2 * D)
        W = jax.random.uniform(k3, (D, 2 * D), minval=-bound, maxval=bound, dtype=jnp.float32)
        b = jax.random.uniform(k4, (D,), minval=-bound, maxval=bound, dtype=jnp.float32)
        alpha = jnp.full((D,), 0.1, dtype=jnp.float32)
        return {'h_t': h_t, 'z': z, 'W': W, 'b': b, 'alpha': alpha}
    _L1_cond_all = _L1_cond_setup()
    _L1_cond_in = {k: v for k, v in _L1_cond_all.items() if k in ('W', 'b', 'alpha')}
    del _L1_cond_all
    return {'x': x, 'cond_1024': cond_1024, 'L0_cond_base_up': _L0_cond_in['base_up'], 'L0_cond_base_down': _L0_cond_in['base_down'], 'L0_cond_ln_gamma': _L0_cond_in['ln_gamma'], 'L0_cond_ln_beta': _L0_cond_in['ln_beta'], 'L0_cond_W1': _L0_cond_in['W1'], 'L0_cond_bias1': _L0_cond_in['bias1'], 'L0_cond_W2': _L0_cond_in['W2'], 'L0_cond_bias2': _L0_cond_in['bias2'], 'L1_cond_W': _L1_cond_in['W'], 'L1_cond_b': _L1_cond_in['b'], 'L1_cond_alpha': _L1_cond_in['alpha']}

def reference(x, cond_1024, L0_cond_base_up, L0_cond_base_down, L0_cond_ln_gamma, L0_cond_ln_beta, L0_cond_W1, L0_cond_bias1, L0_cond_W2, L0_cond_bias2, L1_cond_W, L1_cond_b, L1_cond_alpha):
    import jax
    import jax.numpy as jnp

    def _L0_cond_ref(x, ada_emb, base_up, base_down, ln_gamma, ln_beta, W1, bias1, W2, bias2):
        import jax, jax.numpy as jnp
        import numpy as np
        RANK = 8
        LN_EPS = 1e-05
        B, T, D = x.shape
        R = RANK
        mu = jnp.mean(ada_emb, axis=-1, keepdims=True)
        var = jnp.mean(jnp.square(ada_emb - mu), axis=-1, keepdims=True)
        c = (ada_emb - mu) / jnp.sqrt(var + LN_EPS) * ln_gamma + ln_beta
        h = jax.nn.gelu(c @ W1 + bias1, approximate=False)
        w = h @ W2 + bias2
        a1, b1, a2, b2 = [t.reshape(B, D, R) for t in jnp.split(w, 4, axis=-1)]
        u = jnp.einsum('btd,bdr->btr', x, a2)
        mid = jnp.einsum('btd,dl->btl', x, base_down) + jnp.einsum('btr,blr->btl', u, b2)
        mid = jax.nn.gelu(mid, approximate=False)
        v = jnp.einsum('blr,btl->btr', b1, mid)
        out = jnp.einsum('btl,kl->btk', mid, base_up) + jnp.einsum('bkr,btr->btk', a1, v)
        return x + out

    def _L1_cond_ref(h_t, z, W, b, alpha):
        import jax, jax.numpy as jnp
        import numpy as np
        LATENT = 256
        D = h_t.shape[-1]
        Wh = W[:, :D]
        Wz = W[:, D:]
        leak = 1.0 - alpha

        def step(h, z_t):
            gate = jax.nn.sigmoid(h @ Wh.T + z_t @ Wz.T + b)
            h_new = jnp.tanh(h * leak + gate * z_t)
            return (h_new, h_new)
        _, hs = jax.lax.scan(step, h_t, jnp.swapaxes(z, 0, 1))
        return jnp.swapaxes(hs, 0, 1)
    x = x + _L0_cond_ref(x, cond_1024, L0_cond_base_up, L0_cond_base_down, L0_cond_ln_gamma, L0_cond_ln_beta, L0_cond_W1, L0_cond_bias1, L0_cond_W2, L0_cond_bias2)
    x = x + _L1_cond_ref(cond_1024, x, L1_cond_W, L1_cond_b, L1_cond_alpha)
    return x

_drawn_inputs = setup_inputs


def setup_inputs(seed=0):
    import zlib

    import numpy as np

    out = dict(_drawn_inputs(seed))
    spreads = {'L0_cond_ln_gamma': (1.0, 0.2),
     'L0_cond_ln_beta': (0.0, 0.1),
     'L0_cond_bias1': (0.0, 0.1),
     'L0_cond_bias2': (0.0, 0.1),
     'L1_cond_alpha': (0.10000000149011612, 0.6)}
    factors = {'L0_cond_base_up': 4.124, 'L0_cond_base_down': 3.983, 'L1_cond_W': 8.0, 'L1_cond_b': 8.0}
    for name, (base, spread) in spreads.items():
        noise = np.random.default_rng([zlib.crc32(name.encode()), seed]).standard_normal(out[name].shape)
        drawn = base * np.exp(spread * noise) if base else spread * noise
        out[name] = jnp.asarray(drawn.astype(out[name].dtype))
    for name, factor in factors.items():
        out[name] = (out[name] * factor).astype(out[name].dtype)
    return out
```

```python
from contextlib import ExitStack

import concourse.bass as bass
from concourse import mybir

F32 = mybir.dt.float32
BF16 = mybir.dt.bfloat16
F16 = mybir.dt.float16
ACT = mybir.ActivationFunctionType
ALU = mybir.AluOpType
AX = mybir.AxisListType

P = 128
EPS = 1e-5
VARIANCE = 6


def build(nc, x, cond, base_up, base_down, gamma, beta, W1, bias1, W2, bias2, W, b, alpha, out):
    B, T, D = x.shape
    C = D // P
    R = W2.shape[1] // (4 * D)
    TB = 512 // B
    NBLK = T // TB
    TOK = B * TB
    BG = P // R
    G = B // BG
    HALF = TOK // 2
    TILE_B = P // TB
    TILES = TOK // P
    assert C == 2 and G == 2 and TILES == 4 and NBLK % 2 == 0 and NBLK >= 6

    with ExitStack() as ctx:
        def sb(name, shape, dt=F32):
            return ctx.enter_context(nc.sbuf_tensor(name, shape, dt))

        def bank(name):
            return ctx.enter_context(nc.psum_tensor(name, [P, 512], F32))

        def sem(name):
            return ctx.enter_context(nc.semaphore(name))

        pre_gate = [[bank(f"pre_gate{p}{m}") for m in range(C)] for p in range(2)]
        mlp = [bank(f"mlp{m}") for m in range(C)]
        rank_ps = bank("rank_ps")
        turn = bank("turn")

        ident = sb("ident", [P, P])
        mask = sb("mask", [P, BG, TB])
        w_nat = sb("w_nat", [P, C, 2 * D])
        wT = sb("wT", [P, 2 * C, D])
        wh_rest = sb("wh_rest", [P, C, D])
        wh_part = sb("wh_part", [P, 3, C, D], BF16)
        down = sb("down", [P, C, D])
        up_nat = sb("up_nat", [P, C, D])
        upT = sb("upT", [P, C, D])
        ones_bf = sb("ones_bf", [P, TOK], BF16)
        b_rows = sb("b_rows", [P, D])
        b_rest = sb("b_rest", [P, D])
        b_hi = sb("b_hi", [P, D], BF16)
        b_mid = sb("b_mid", [P, D], BF16)
        b_part = sb("b_part", [P, D], BF16)
        w1 = sb("w1", [P, C, D])
        w2 = sb("w2", [P, C, 4, D * R])
        bias2_sb = sb("bias2_sb", [P, D * R])
        w_all = sb("w_all", [P, D * R])
        adapt = sb("adapt", [P, 4, C, G, BG, R])
        a1T = sb("a1T", [P, G, D])
        b2T = sb("b2T", [P, G, D])
        cond_sb = sb("cond_sb", [B, D])
        cond_sq = sb("cond_sq", [B, D])
        cond_n = sb("cond_n", [B, D])
        stat = sb("stat", [B, 8])
        cols = sb("cols", [P, 4, C])
        leak_col = sb("leak_col", [P, C])
        condT = sb("condT", [P, C, B])
        cT = sb("cT", [P, C, B])
        hidT0 = sb("hidT0", [P, C, B])
        x_nat = sb("x_nat", [P, 2, TILES, D])
        xT = sb("xT", [P, 2, C, TOK])
        u_sb = sb("u_sb", [P, G, HALF])
        v_sb = sb("v_sb", [P, G, HALF])
        hid = sb("hid", [P, C, TOK])
        zp = sb("zp", [P, 2, C, TB, B, 2])
        h_all = sb("h_all", [P, 2, C, TB, B])
        yT = sb("yT", [P, 2, C, TOK])
        y_nat = sb("y_nat", [P, 2, TILES, D])
        gl = sb("gl", [P, C, B, 2])
        pre = sb("pre", [P, C, B, 2])
        h_hi = sb("h_hi", [P, C, B], F16)
        h_lo = sb("h_lo", [P, C, B], F16)

        s_small, s_w, s_base, s_w1, s_bias2, s_x0 = (sem(n) for n in (
            "small_landed", "w_landed", "base_landed", "w1_landed", "bias2_landed", "cond_landed"))
        s_w2 = [sem(f"w2_landed{j}") for j in range(4)]
        s_zero = sem("zeroed")
        s_ident, s_mask = sem("ident_ready"), sem("mask_ready")
        s_dve, s_act = sem("dve_chain"), sem("act_chain")
        s_prep_pe, s_prep_ev = sem("prep_matmul"), sem("prep_evacuated")
        s_wgen, s_wev = sem("adapters_made"), sem("adapters_copied")
        s_normed = sem("conditioning_normed")
        s_hid0 = sem("adapter_hidden_ready")
        x_landed = [sem(f"x_landed{p}") for p in range(2)]
        y_stored = [sem(f"y_stored{p}") for p in range(2)]
        x_turned, x_copied = sem("x_turned"), sem("x_copied")
        y_turned, y_copied = sem("y_turned"), sem("y_copied")
        u_made, u_masked = sem("u_made"), sem("u_masked")
        v_made, v_masked = sem("v_made"), sem("v_masked")
        mid_made, hid_made = sem("mid_made"), sem("hid_made")
        mlp_made, z_made = sem("mlp_made"), sem("z_made")
        z_doubled, y_made = sem("z_doubled"), sem("y_made")
        gate_in, gate_out = sem("gate_in"), sem("gate_out")
        pre_made = sem("pre_made")
        hi_made, h_made, lo_made = sem("hi_made"), sem("h_made"), sem("lo_made")
        leaked = sem("leaked")

        def wait(eng, s, value):
            if not isinstance(value, int) or value > 0:
                eng.wait_ge(s, value)

        def landed(n, p):
            return 8 * TILES * (n - p) + 16 * TILES

        def each_block(eng, body):
            for n in (0, 1):
                body(n, n, 0, n + 2 < NBLK, True, n >= 1)
            with eng.Fori(1, NBLK // 2 - 1) as i:
                for p in range(2):
                    body(2 * i + p, p, i, True, True, True)
            for n in (NBLK - 2, NBLK - 1):
                body(n, n % 2, n // 2, False, n + 1 < NBLK, True)

        block = ctx.enter_context(nc.Block())

        @block.sync
        def _(sp):
            def load_x(n, p):
                for q in range(TILES):
                    sp.dma_start(x_nat[:, p, q, :],
                                 x[q * TILE_B:(q + 1) * TILE_B, bass.ds(n * TB, TB), :]
                                 ).then_inc(x_landed[p], 16)

            def store_y(n, p, half):
                for q in (2 * half, 2 * half + 1):
                    sp.dma_start(out[q * TILE_B:(q + 1) * TILE_B, bass.ds(n * TB, TB), :],
                                 y_nat[:, p, q, :]).then_inc(y_stored[p], 16)

            sp.dma_start(cond_sb[:, :], cond).then_inc(s_x0, 16)
            for i, v in enumerate((gamma, beta, bias1, alpha)):
                sp.dma_start(cols[:, i, :], v.rearrange("(c p) -> p c", p=P),
                             allow_slow_non_contiguous=True).then_inc(s_small, 16)
            sp.wait_ge(s_zero, 1)
            for i in range(3):
                sp.dma_start(b_rows[32 * i:32 * i + 1, :], b.rearrange("(a d) -> a d", a=1)).then_inc(s_small, 16)
            sp.dma_start(w1[:, :, :], W1.rearrange("(c p) n -> p c n", p=P)).then_inc(s_w1, 16)
            w2_v = W2.rearrange("(c p) (q n) -> p c q n", p=P, q=4)
            for j in range(4):
                for c in range(C):
                    sp.dma_start(w2[:, c, :, j * 512:(j + 1) * 512],
                                 w2_v[:, c, :, j * 512:(j + 1) * 512]).then_inc(s_w2[j], 16)
                if j == 1:
                    load_x(0, 0)
            load_x(1, 1)

            def body(n, p, i, front, mid, back):
                if front:
                    wait(sp, x_turned, 2 * (n + 1))
                    load_x(n + 2, p)
                if back:
                    for half in range(2):
                        wait(sp, y_copied, 4 * (n - 1) + 2 * half + 2)
                        store_y(n - 1, 1 - p, half)

            each_block(sp, body)
            for half in range(2):
                sp.wait_ge(y_copied, 4 * (NBLK - 1) + 2 * half + 2)
                store_y(NBLK - 1, (NBLK - 1) % 2, half)
            for p in range(2):
                sp.wait_ge(y_stored[p], 16 * TILES * NBLK // 2)

        @block.gpsimd
        def _(pool):
            for c in range(C):
                pool.dma_start(w_nat[:, c, :], W[c * P:(c + 1) * P, :]).then_inc(s_w, 16)
            pool.dma_start(down[:, :, :], base_down.rearrange("(c p) n -> p c n", p=P)).then_inc(s_base, 16)
            pool.dma_start(up_nat[:, :, :], base_up.rearrange("(c p) n -> p c n", p=P)).then_inc(s_base, 16)
            bias2_v = bias2.rearrange("(q o n) -> q o n", q=4, o=1)
            for q in range(4):
                pool.dma_start(bias2_sb[q * B:(q + 1) * B, :],
                               bias2_v[q].broadcast_to([B, D * R])).then_inc(s_bias2, 16)
            pool.memset(ident[:, :], 0.0).then_inc(s_ident, 1)
            pool.wait_ge(s_ident, 1)
            pool.affine_select(out=ident[:, :], in_=ident[:, :], compare_op=ALU.not_equal, fill=1.0,
                               base=0, pattern=[[-1, P]], channel_multiplier=1).then_inc(s_ident, 1)
            pool.memset(mask[:, :, :], 1.0).then_inc(s_mask, 1)
            pool.wait_ge(s_mask, 1)
            pool.affine_select(out=mask[:, :, :], in_=mask[:, :, :], compare_op=ALU.is_ge, fill=0.0,
                               base=0, pattern=[[-R, BG], [0, TB]], channel_multiplier=1).then_inc(s_mask, 1)
            pool.wait_ge(s_mask, 2)
            pool.affine_select(out=mask[:, :, :], in_=mask[:, :, :], compare_op=ALU.is_ge, fill=0.0,
                               base=R - 1, pattern=[[R, BG], [0, TB]], channel_multiplier=-1).then_inc(s_mask, 1)

            def body(n, p, i, front, mid, back):
                wait(pool, y_turned, 2 * (n - 1))
                pool.wait_ge(z_made, 4 * (n + 1))
                for c in range(C):
                    zh = zp[:, p, c, :, :, 1].rearrange("p s b -> p b s")
                    pool.tensor_tensor(yT[:, p, c, :].rearrange("p (b s) -> p b s", b=B),
                                       zh, zh, ALU.add).then_inc(z_doubled, 1)
                pool.wait_ge(z_doubled, 2 * (n + 1))
                for half in range(2):
                    pool.wait_ge(h_made, 2 * TB * n + TB * (half + 1))
                    s0, s1 = half * TB // 2, (half + 1) * TB // 2
                    for c in range(C):
                        y = yT[:, p, c, :].rearrange("p (b s) -> p b s", b=B)[:, :, s0:s1]
                        pool.tensor_tensor(
                            y, y, h_all[:, p, c, s0:s1, :].rearrange("p s b -> p b s"),
                            ALU.add).then_inc(y_made, 1)

            each_block(nc.gpsimd, body)

        @block.tensor
        def _(pe):
            def turn_x(n, p, half):
                if half == 0:
                    pe.wait_ge(x_landed[p], landed(n, p))
                    wait(pe, x_copied, 4 * n)
                    wait(pe, y_copied, 4 * (n - 3))
                else:
                    pe.wait_ge(x_copied, 4 * n + 2)
                for c in range(C):
                    for q in range(2):
                        mm = pe.transpose(turn[:, (2 * c + q) * P:(2 * c + q + 1) * P],
                                          x_nat[:, p, 2 * half + q, c * P:(c + 1) * P], ident[:, :])
                mm.then_inc(x_turned, 1)

            def turn_y(n, p, half):
                if half == 0:
                    wait(pe, x_copied, 4 * min(n + 4, NBLK) if isinstance(n, int) else 4 * (n + 4))
                    pe.wait_ge(y_made, 4 * (n + 1))
                else:
                    pe.wait_ge(y_copied, 4 * n + 2)
                for q in range(2):
                    for c in range(C):
                        t0 = (2 * half + q) * P
                        mm = pe.transpose(turn[:, (2 * q + c) * P:(2 * q + c + 1) * P],
                                          yT[:, p, c, t0:t0 + P], ident[:, :])
                mm.then_inc(y_turned, 1)

            def project_x(n, p, g):
                if g == 0:
                    pe.wait_ge(x_copied, 4 * (n + 1))
                    wait(pe, v_masked, 2 * n)
                for k in range(C):
                    mm = pe.matmul(rank_ps[:, g * HALF:(g + 1) * HALF],
                                   adapt[:, 2, k, g, :, :].rearrange("p b r -> p (b r)"),
                                   xT[:, p, k, g * HALF:(g + 1) * HALF], start=(k == 0), stop=(k == C - 1))
                if g == G - 1:
                    mm.then_inc(u_made, 1)

            def project_hid(n, g):
                if g == 0:
                    pe.wait_ge(u_masked, 2 * (n + 1))
                    pe.wait_ge(hid_made, 4 * (n + 1))
                for k in range(C):
                    mm = pe.matmul(rank_ps[:, g * HALF:(g + 1) * HALF],
                                   adapt[:, 1, k, g, :, :].rearrange("p b r -> p (b r)"),
                                   hid[:, k, g * HALF:(g + 1) * HALF], start=(k == 0), stop=(k == C - 1))
                if g == G - 1:
                    mm.then_inc(v_made, 1)

            def down_base(n, p, m, k):
                if k == 0:
                    wait(pe, z_made, 4 * (n - 1) + 2 * (m + 1))
                pe.matmul(mlp[m][:, :], down[:, k, m * P:(m + 1) * P], xT[:, p, k, :],
                          start=(k == 0), stop=False, skip_group_check=True)

            def down_adapter(n, m):
                pe.wait_ge(u_masked, 2 * (n + 1))
                for g in range(G):
                    mm = pe.matmul(mlp[m][:, g * HALF:(g + 1) * HALF], b2T[:, g, m * P:(m + 1) * P],
                                   u_sb[:, g, :], start=False, stop=(g == G - 1), skip_group_check=True)
                mm.then_inc(mid_made, 1)

            def up_base(n, m, k):
                pe.matmul(mlp[m][:, :], upT[:, k, m * P:(m + 1) * P], hid[:, k, :],
                          start=(k == 0), stop=False, skip_group_check=True)

            def up_adapter(n, m):
                pe.wait_ge(v_masked, 2 * (n + 1))
                for g in range(G):
                    mm = pe.matmul(mlp[m][:, g * HALF:(g + 1) * HALF], a1T[:, g, m * P:(m + 1) * P],
                                   v_sb[:, g, :], start=False, stop=(g == G - 1), skip_group_check=True)
                mm.then_inc(mlp_made, 1)

            def gate_bias(n, p, m):
                wait(pe, gate_out, 2 * TB * (n - 1))
                pe.matmul(pre_gate[p][m][:, :], b_part[:, m * P:(m + 1) * P], ones_bf[:, :],
                          start=True, stop=False, skip_group_check=True)

            def gate_z(n, p, m, k):
                pe.wait_ge(z_made, 4 * n + 2 * (k + 1))
                pe.matmul(pre_gate[p][m][:, :], wT[:, C + k, m * P:(m + 1) * P],
                          zp[:, p, k, :, :, 1].rearrange("p s b -> p (s b)"),
                          start=False, stop=False, skip_group_check=True)

            def first_half(n, p):
                turn_x(n, p, 0)
                turn_x(n, p, 1)
                for g in range(G):
                    project_x(n, p, g)
                for m in range(C):
                    for k in range(C):
                        down_base(n, p, m, k)
                    down_adapter(n, m)

            def second_half(n, p):
                for g in range(G):
                    project_hid(n, g)
                for m in range(C):
                    for k in range(C):
                        up_base(n, m, k)
                    up_adapter(n, m)
                for m in range(C):
                    gate_bias(n, p, m)
                for k in range(C):
                    for m in range(C):
                        gate_z(n, p, m, k)

            def side_work(s, n, p, front, mid, back):
                q = 1 - p
                if mid:
                    if s in (0, 1):
                        project_hid(n + 1, s)
                    if s in (2, 3):
                        up_base(n + 1, 0, s - 2)
                    if s == 4:
                        up_base(n + 1, 1, 0)
                        up_adapter(n + 1, 0)
                    if s == 5:
                        up_base(n + 1, 1, 1)
                    if s == 6:
                        up_adapter(n + 1, 1)
                if front:
                    if s == 0:
                        turn_x(n + 2, p, 0)
                    if s == 3:
                        turn_x(n + 2, p, 1)
                    if s in (6, 7):
                        project_x(n + 2, p, s - 6)
                    if s in (8, 9):
                        down_base(n + 2, p, 0, s - 8)
                    if s == 10:
                        down_base(n + 2, p, 1, 0)
                        down_adapter(n + 2, 0)
                    if s == 11:
                        down_base(n + 2, p, 1, 1)
                    if s == 12:
                        down_adapter(n + 2, 1)
                if back:
                    if s == 6:
                        turn_y(n - 1, q, 0)
                    if s == 9:
                        turn_y(n - 1, q, 1)
                if mid:
                    if s == 7:
                        gate_bias(n + 1, q, 0)
                        gate_bias(n + 1, q, 1)
                    if s == 12:
                        gate_z(n + 1, q, 0, 0)
                    if s == 13:
                        gate_z(n + 1, q, 1, 0)
                    if s == 14:
                        gate_z(n + 1, q, 0, 1)
                    if s == 15:
                        gate_z(n + 1, q, 1, 1)

            def step(n, p, s):
                if not (isinstance(n, int) and n == 0 and s == 0):
                    done = 2 * (TB * n + s) - 2
                    for k in range(C):
                        pe.wait_ge(hi_made, done + k + 1)
                        for m in range(C):
                            for w in range(3):
                                pe.matmul(pre_gate[p][m][:, s * B:(s + 1) * B],
                                          wh_part[:, w, k, m * P:(m + 1) * P], h_hi[:, k, :],
                                          start=False, stop=False, skip_group_check=True)
                    for k in range(C):
                        pe.wait_ge(lo_made, done + k + 1)
                        for m in range(C):
                            for w in range(3):
                                mm = pe.matmul(pre_gate[p][m][:, s * B:(s + 1) * B],
                                               wh_part[:, w, k, m * P:(m + 1) * P], h_lo[:, k, :],
                                               start=False, stop=(k == C - 1 and w == 2),
                                               skip_group_check=True)
                            if k == C - 1:
                                mm.then_inc(gate_in, 1)

            def turned(dst, src, n_in=P):
                pe.transpose(dst, src, ident[0:n_in, 0:n_in]).then_inc(s_prep_pe, 1)

            pe.wait_ge(s_ident, 2)
            pe.wait_ge(s_normed, 1)
            for c in range(C):
                turned(turn[:, c * B:(c + 1) * B], cond_sb[:, c * P:(c + 1) * P], B)
            for c in range(C):
                turned(turn[:, (C + c) * B:(C + c + 1) * B], cond_n[:, c * P:(c + 1) * P], B)
            pe.wait_ge(s_w1, 16)
            pe.wait_ge(s_prep_ev, 1)
            for m in range(C):
                for k in range(C):
                    mm = pe.matmul(mlp[0][:, m * B:(m + 1) * B], w1[:, k, m * P:(m + 1) * P], cT[:, k, :],
                                   start=(k == 0), stop=(k == C - 1))
            mm.then_inc(s_prep_pe, 1)
            pe.wait_ge(s_w, 16 * C)
            for i in range(2 * C):
                bnk = (mlp[1], rank_ps)[i // 2]
                for j in range(C):
                    c0 = ((i % 2) * C + j) * P
                    mm = pe.transpose(bnk[:, c0:c0 + P], w_nat[:, j, i * P:(i + 1) * P], ident[:, :])
                if i % 2:
                    mm.then_inc(s_prep_pe, 1)
            pe.wait_ge(s_base, 32)
            pe.wait_ge(s_prep_ev, 1)
            for i in range(C):
                for j in range(C):
                    mm = pe.transpose(turn[:, (i * C + j) * P:(i * C + j + 1) * P],
                                      up_nat[:, j, i * P:(i + 1) * P], ident[:, :])
            mm.then_inc(s_prep_pe, 1)
            pe.wait_ge(s_hid0, 1)
            pe.wait_ge(s_prep_ev, 3)
            wbank = [mlp[0], mlp[1], rank_ps, pre_gate[0][0]]
            for j in range(4):
                pe.wait_ge(s_w2[j], 16 * C)
                for k in range(C):
                    for q in range(4):
                        mm = pe.matmul(wbank[j][q * B:(q + 1) * B, :], hidT0[:, k, :],
                                       w2[:, k, q, j * 512:(j + 1) * 512],
                                       start=(k == 0), stop=(k == C - 1), tile_position=(0, q * B))
                mm.then_inc(s_wgen, 1)
            tb = [turn, pre_gate[0][1], pre_gate[1][0], pre_gate[1][1]]
            pe.wait_ge(s_prep_ev, 4)
            for c in range(C):
                pe.wait_ge(s_wev, 2 * (c + 1))
                wv = w_all[:, :].rearrange("p (d r) -> p d r", r=R)
                for rh in range(2):
                    for r in range(4):
                        mm = pe.transpose(tb[2 * c + rh][:, r * P:(r + 1) * P],
                                          wv[:, c * P:(c + 1) * P, 4 * rh + r], ident[:, :])
                    mm.then_inc(s_wgen, 1)
            pe.wait_ge(s_wev, 4 + 16)
            for i, (q, bnk) in enumerate(((0, mlp[0]), (3, mlp[1]))):
                for g in range(G):
                    for c in range(C):
                        c0 = (g * C + c) * P
                        mm = pe.transpose(bnk[:, c0:c0 + P],
                                          adapt[:, q, c, g, :, :].rearrange("p b r -> p (b r)"), ident[:, :])
                mm.then_inc(s_wgen, 1)
            pe.wait_ge(s_wev, 4 + 16 + 2)
            first_half(0, 0)
            second_half(0, 0)
            for m in range(C):
                for k in range(C):
                    mm = pe.matmul(pre_gate[0][m][:, 0:B], wT[:, k, m * P:(m + 1) * P], condT[:, k, :],
                                   start=False, stop=(k == C - 1), skip_group_check=True)
                mm.then_inc(gate_in, 1)
            first_half(1, 1)

            def body(n, p, i, front, mid, back):
                for s in range(TB):
                    step(n, p, s)
                    side_work(s, n, p, front, mid, back)

            each_block(nc.tensor, body)
            turn_y(NBLK - 1, (NBLK - 1) % 2, 0)
            turn_y(NBLK - 1, (NBLK - 1) % 2, 1)

        @block.scalar
        def _(act):
            def copy_x(n, p, half, c):
                if c == 0:
                    act.wait_ge(x_turned, 2 * n + half + 1)
                    wait(act, z_made, 4 * (n - 1))
                act.activation(xT[:, p, c, half * HALF:(half + 1) * HALF],
                               turn[:, c * HALF:(c + 1) * HALF], ACT.Copy).then_inc(x_copied, 1)

            def copy_y(n, p, half, q):
                if q == 0:
                    act.wait_ge(y_turned, 2 * n + half + 1)
                    if half == 0:
                        wait(act, y_stored[p], 8 * TILES * (n - p))
                act.activation(y_nat[:, p, 2 * half + q, :], turn[:, q * D:(q + 1) * D],
                               ACT.Copy).then_inc(y_copied, 1)

            def gelu_piece(n, m, half):
                if half == 0:
                    act.wait_ge(mid_made, 2 * n + m + 1)
                c0 = half * HALF
                act.activation(hid[:, m, c0:c0 + HALF], mlp[m][:, c0:c0 + HALF],
                               ACT.Gelu).then_inc(hid_made, 1)

            def step(n, p, s):
                t2 = 2 * (TB * n + s)
                for c in range(C):
                    act.wait_ge(gate_in, t2 + c + 1)
                    act.activation(gl[:, c, :, 0], pre_gate[p][c][:, s * B:(s + 1) * B],
                                   ACT.Tanh, scale=0.5).then_inc(gate_out, 1)
                for c in range(C):
                    act.wait_ge(pre_made, t2 + c + 1)
                    act.activation(h_hi[:, c, :], pre[:, c, :, 1], ACT.Tanh).then_inc(hi_made, 1)
                    act.activation(h_all[:, p, c, s, :], pre[:, c, :, 1], ACT.Tanh).then_inc(h_made, 1)

            def side_work(s, n, p, front, mid, back):
                q = 1 - p
                if front:
                    if s in (1, 2):
                        copy_x(n + 2, p, 0, s - 1)
                    if s in (4, 5):
                        copy_x(n + 2, p, 1, s - 4)
                    if s in (11, 12):
                        gelu_piece(n + 2, 0, s - 11)
                    if s in (13, 14):
                        gelu_piece(n + 2, 1, s - 13)
                if back:
                    if s in (7, 8):
                        copy_y(n - 1, q, 0, s - 7)
                    if s in (9, 10):
                        copy_y(n - 1, q, 1, s - 9)

            act.wait_ge(s_dve, VARIANCE)
            act.activation(stat[:, 3:4], stat[:, 2:3], ACT.Sqrt).then_inc(s_act, 1)
            act.wait_ge(s_prep_pe, 5)
            for m in range(C):
                last = act.activation(hidT0[:, m, :], mlp[0][:, m * B:(m + 1) * B], ACT.Gelu,
                                      bias=cols[:, 2, m:m + 1])
            last.then_inc(s_hid0, 1)
            for n in range(2):
                for half in range(2):
                    for c in range(C):
                        copy_x(n, n, half, c)
                for m in range(C):
                    for half in range(2):
                        gelu_piece(n, m, half)

            def body(n, p, i, front, mid, back):
                wait(act, y_made, 4 * (n - 1))
                for s in range(TB):
                    step(n, p, s)
                    side_work(s, n, p, front, mid, back)

            each_block(nc.scalar, body)
            for half in range(2):
                for q in range(2):
                    copy_y(NBLK - 1, (NBLK - 1) % 2, half, q)

        @block.vector
        def _(dve):
            def mask_piece(n, made, masked, dst, g):
                if g == 0:
                    dve.wait_ge(made, n + 1)
                dve.tensor_tensor(dst[:, g, :], rank_ps[:, g * HALF:(g + 1) * HALF],
                                  mask[:, :, :].rearrange("p b s -> p (b s)"), ALU.mult).then_inc(masked, 1)

            def z_piece(n, p, m, g):
                if g == 0:
                    dve.wait_ge(mlp_made, 2 * n + m + 1)
                    if m == 0:
                        wait(dve, y_made, 4 * (n - 1))
                c0 = g * HALF
                dve.scalar_tensor_tensor(
                    zp[:, p, m, :, g * BG:(g + 1) * BG, 1].rearrange("p s b -> p b s"),
                    mlp[m][:, c0:c0 + HALF].rearrange("p (b s) -> p b s", b=BG), 0.5,
                    xT[:, p, m, c0:c0 + HALF].rearrange("p (b s) -> p b s", b=BG),
                    ALU.mult, ALU.add).then_inc(z_made, 1)

            def leak_h(c, state, p, s):
                dve.scalar_tensor_tensor(gl[:, c, :, 1], state, leak_col[:, c:c + 1],
                                         zp[:, p, c, s, :, 1], ALU.mult, ALU.add).then_inc(leaked, 1)

            def step(n, p, s):
                t = TB * n + s
                for c in range(C):
                    dve.wait_ge(gate_out, 2 * t + c + 1)
                    dve.wait_ge(leaked, 2 * t + c + 1)
                    dve.tensor_tensor_scan(pre[:, c, :, :].rearrange("p b j -> p (b j)"),
                                           zp[:, p, c, s, :, :].rearrange("p b j -> p (b j)"),
                                           gl[:, c, :, :].rearrange("p b j -> p (b j)"),
                                           0.0, ALU.mult, ALU.add).then_inc(pre_made, 1)
                for c in range(C):
                    dve.wait_ge(h_made, 2 * t + c + 1)
                    dve.tensor_tensor(h_lo[:, c, :], h_all[:, p, c, s, :], h_hi[:, c, :],
                                      ALU.subtract).then_inc(lo_made, 1)
                if not (isinstance(n, int) and t == T - 1):
                    if s == TB - 1:
                        dve.wait_ge(z_made, 4 * (n + 2))
                    for c in range(C):
                        leak_h(c, h_all[:, p, c, s, :], *((p, s + 1) if s < TB - 1 else (1 - p, 0)))

            def side_work(s, n, p, front, mid, back):
                q = 1 - p
                if mid:
                    if s in (2, 3):
                        mask_piece(n + 1, v_made, v_masked, v_sb, s - 2)
                    if s in (5, 6):
                        z_piece(n + 1, q, 0, s - 5)
                    if s in (7, 8):
                        z_piece(n + 1, q, 1, s - 7)
                if front:
                    if s in (9, 10):
                        mask_piece(n + 2, u_made, u_masked, u_sb, s - 9)

            chain = [0]

            def link(ins):
                chain[0] += 1
                ins.then_inc(s_dve, 1)
                dve.wait_ge(s_dve, chain[0])

            dve.memset(b_rows[:, :], 0.0).then_inc(s_zero, 1)
            dve.wait_ge(s_x0, 16)
            link(dve.tensor_reduce(stat[:, 0:1], cond_sb[:, :], AX.X, ALU.add))
            link(dve.tensor_scalar(stat[:, 1:2], stat[:, 0:1], 1.0 / D, None, ALU.mult))
            link(dve.tensor_scalar(cond_n[:, :], cond_sb[:, :], stat[:, 1:2], None, ALU.subtract))
            link(dve.tensor_tensor(cond_sq[:, :], cond_n[:, :], cond_n[:, :], ALU.mult))
            link(dve.tensor_reduce(stat[:, 5:6], cond_sq[:, :], AX.X, ALU.add))
            link(dve.tensor_scalar(stat[:, 2:3], stat[:, 5:6], 1.0 / D, EPS, ALU.mult, ALU.add))
            dve.wait_ge(s_act, 1)
            link(dve.reciprocal(stat[:, 4:5], stat[:, 3:4]))
            dve.tensor_scalar(cond_n[:, :], cond_n[:, :], stat[:, 4:5], None, ALU.mult).then_inc(s_normed, 1)
            dve.wait_ge(s_small, 16 * 7)
            dve.wait_ge(s_prep_pe, 4)
            dve.tensor_copy(condT[:, :, :].rearrange("p c b -> p (c b)"), turn[:, 0:C * B])
            for c in range(C):
                last = dve.tensor_scalar(cT[:, c, :], turn[:, (C + c) * B:(C + c + 1) * B],
                                         cols[:, 0, c:c + 1], cols[:, 1, c:c + 1], ALU.mult, ALU.add)
            last.then_inc(s_prep_ev, 1)
            link(dve.memset(ones_bf[:, :], 1.0))
            link(dve.memset(zp[:, :, :, :, :, :].rearrange("p a c s b j -> p (a c s b j)"), 0.0))
            link(dve.tensor_scalar(leak_col[:, :], cols[:, 3, :], -1.0, 1.0, ALU.mult, ALU.add))
            dve.wait_ge(s_prep_pe, 7)
            dve.tensor_copy(wT[:, 0:C, :].rearrange("p c n -> p (c n)"), mlp[1][:, :]).then_inc(s_prep_ev, 1)
            dve.tensor_scalar(wT[:, C:2 * C, :].rearrange("p c n -> p (c n)"), rank_ps[:, :], 2.0, None,
                              ALU.mult).then_inc(s_prep_ev, 1)
            dve.wait_ge(s_prep_pe, 8)
            dve.tensor_copy(upT[:, :, :].rearrange("p c n -> p (c n)"), turn[:, :]).then_inc(s_prep_ev, 1)
            dve.wait_ge(s_prep_ev, 2)
            link(dve.tensor_copy(wh_part[:, 0, :, :], wT[:, 0:C, :]))
            link(dve.tensor_tensor(wh_rest[:, :, :], wT[:, 0:C, :], wh_part[:, 0, :, :], ALU.subtract))
            link(dve.tensor_copy(wh_part[:, 1, :, :], wh_rest[:, :, :]))
            link(dve.tensor_tensor(wh_part[:, 2, :, :], wh_rest[:, :, :], wh_part[:, 1, :, :], ALU.subtract))
            link(dve.memset(b_part[:, :], 0.0))
            link(dve.tensor_copy(b_hi[:, :], b_rows[:, :]))
            link(dve.tensor_tensor(b_rest[:, :], b_rows[:, :], b_hi[:, :], ALU.subtract))
            link(dve.tensor_copy(b_mid[:, :], b_rest[:, :]))
            link(dve.tensor_copy(b_part[0:1, :], b_hi[0:1, :]))
            link(dve.tensor_copy(b_part[32:33, :], b_mid[32:33, :]))
            link(dve.tensor_tensor(b_part[64:65, :], b_rest[64:65, :], b_mid[64:65, :], ALU.subtract))
            dve.wait_ge(s_bias2, 16 * 4)
            wbank = [mlp[0], mlp[1], rank_ps, pre_gate[0][0]]
            for j in range(4):
                dve.wait_ge(s_wgen, j + 1)
                dve.tensor_tensor(w_all[:, j * 512:(j + 1) * 512], wbank[j][:, :],
                                  bias2_sb[:, j * 512:(j + 1) * 512], ALU.add).then_inc(s_wev, 1)
            tb = [turn, pre_gate[0][1], pre_gate[1][0], pre_gate[1][1]]
            for c in range(C):
                for rh in range(2):
                    dve.wait_ge(s_wgen, 5 + 2 * c + rh)
                    for q in range(4):
                        src = tb[2 * c + rh][:, :].rearrange("p (r q g b) -> p q r g b", r=4, q=4, g=G)[:, q]
                        dst = adapt[:, q, c, :, :, 4 * rh:4 * rh + 4].rearrange("p g b r -> p r g b")
                        dve.tensor_copy(dst, src).then_inc(s_wev, 1)
            for i, (dst, bnk) in enumerate(((a1T, mlp[0]), (b2T, mlp[1]))):
                dve.wait_ge(s_wgen, 9 + i)
                dve.tensor_copy(dst[:, :, :].rearrange("p g n -> p (g n)"), bnk[:, :]).then_inc(s_wev, 1)
            dve.wait_ge(s_mask, 3)
            for n in range(2):
                for g in range(G):
                    mask_piece(n, u_made, u_masked, u_sb, g)
                if n == 0:
                    for g in range(G):
                        mask_piece(n, v_made, v_masked, v_sb, g)
                    for m in range(C):
                        for g in range(G):
                            z_piece(n, n, m, g)
                    dve.wait_ge(z_made, 4)
                    for c in range(C):
                        leak_h(c, condT[:, c, :], 0, 0)

            def body(n, p, i, front, mid, back):
                for s in range(TB):
                    step(n, p, s)
                    side_work(s, n, p, front, mid, back)

            each_block(nc.vector, body)


_INS = ["x", "cond_1024", "L0_cond_base_up", "L0_cond_base_down", "L0_cond_ln_gamma", "L0_cond_ln_beta",
        "L0_cond_W1", "L0_cond_bias1", "L0_cond_W2", "L0_cond_bias2", "L1_cond_W", "L1_cond_b",
        "L1_cond_alpha"]


def kernel(**inputs):
    import numpy as np
    import concourse.bacc as bacc
    from concourse.bass_utils import run_bass_kernel_spmd

    nc = bacc.Bacc("TRN2", target_bir_lowering=False, num_devices=1)
    arrays, args = {}, []
    for name in _INS:
        a = np.ascontiguousarray(inputs[name])
        arrays[f"in_{name}"] = a
        args.append(nc.dram_tensor(f"in_{name}", a.shape, mybir.dt.from_np(a.dtype), kind="ExternalInput").ap())
    shape = inputs["x"].shape
    args.append(nc.dram_tensor("out_0", shape, F32, kind="ExternalOutput").ap())
    build(nc, *args)
    r = run_bass_kernel_spmd(nc, [arrays], core_ids=[0])
    return r.results[0]["out_0"]
```

```python
from contextlib import ExitStack

import concourse.bass as bass
from concourse import mybir

F32 = mybir.dt.float32
BF16 = mybir.dt.bfloat16
F16 = mybir.dt.float16
ACT = mybir.ActivationFunctionType
ALU = mybir.AluOpType
AX = mybir.AxisListType

P = 128
EPS = 1e-5
VARIANCE = 6


def build(nc, x, cond, base_up, base_down, gamma, beta, W1, bias1, W2, bias2, W, b, alpha, out):
    B, T, D = x.shape
    C = D // P
    R = W2.shape[1] // (4 * D)
    TB = 512 // B
    NBLK = T // TB
    TOK = B * TB
    BG = P // R
    G = B // BG
    HALF = TOK // 2
    TILE_B = P // TB
    TILES = TOK // P
    assert C == 2 and G == 2 and TILES == 4 and NBLK % 2 == 0 and NBLK >= 6

    with ExitStack() as ctx:
        def sb(name, shape, dt=F32):
            return ctx.enter_context(nc.sbuf_tensor(name, shape, dt))

        def bank(name):
            return ctx.enter_context(nc.psum_tensor(name, [P, 512], F32))

        def sem(name):
            return ctx.enter_context(nc.semaphore(name))

        pre_gate = [[bank(f"pre_gate{p}{m}") for m in range(C)] for p in range(2)]
        mlp = [bank(f"mlp{m}") for m in range(C)]
        rank_ps = bank("rank_ps")
        turn = bank("turn")

        ident = sb("ident", [P, P])
        mask = sb("mask", [P, TILE_B, TB])
        w_nat = sb("w_nat", [P, C, 2 * D])
        wT = sb("wT", [P, 2 * C, D])
        wh_rest = sb("wh_rest", [P, C, D])
        wh_part = sb("wh_part", [P, 3, C, D], BF16)
        down = sb("down", [P, C, D])
        up_nat = sb("up_nat", [P, C, D])
        upT = sb("upT", [P, C, D])
        ones_bf = sb("ones_bf", [P, TOK], BF16)
        b_rows = sb("b_rows", [P, D])
        b_rest = sb("b_rest", [P, D])
        b_hi = sb("b_hi", [P, D], BF16)
        b_mid = sb("b_mid", [P, D], BF16)
        b_part = sb("b_part", [P, D], BF16)
        w1 = sb("w1", [P, C, D])
        w2 = sb("w2", [P, C, 4, D * R])
        bias2_sb = sb("bias2_sb", [P, D * R])
        w_all = sb("w_all", [P, D * R])
        adapt = sb("adapt", [P, 4, C, G, BG, R])
        a1T = sb("a1T", [P, G, D])
        b2T = sb("b2T", [P, G, D])
        cond_sb = sb("cond_sb", [B, D])
        cond_sq = sb("cond_sq", [B, D])
        cond_n = sb("cond_n", [B, D])
        stat = sb("stat", [B, 8])
        cols = sb("cols", [P, 4, C])
        leak_col = sb("leak_col", [P, C])
        condT = sb("condT", [P, C, B])
        cT = sb("cT", [P, C, B])
        hidT0 = sb("hidT0", [P, C, B])
        x_nat = sb("x_nat", [P, 2, TILES, D])
        xT = sb("xT", [P, 2, C, TOK])
        u_sb = sb("u_sb", [P, G, 2, P])
        v_sb = sb("v_sb", [P, G, 2, P])
        hid = sb("hid", [P, C, TOK])
        zp = sb("zp", [P, 2, C, TB, B, 2])
        h_all = sb("h_all", [P, 2, C, TB, B])
        yT = sb("yT", [P, 2, C, TOK])
        y_nat = sb("y_nat", [P, 2, TILES, D])
        gl = sb("gl", [P, C, B, 2])
        pre = sb("pre", [P, C, B, 2])
        h_hi = sb("h_hi", [P, C, B], F16)
        h_lo = sb("h_lo", [P, C, B], F16)

        s_small, s_w, s_base, s_w1, s_bias2, s_x0 = (sem(n) for n in (
            "small_landed", "w_landed", "base_landed", "w1_landed", "bias2_landed", "cond_landed"))
        s_w2 = [sem(f"w2_landed{j}") for j in range(4)]
        s_zero = sem("zeroed")
        s_ident, s_mask = sem("ident_ready"), sem("mask_ready")
        s_dve, s_act = sem("dve_chain"), sem("act_chain")
        s_prep_pe, s_prep_ev = sem("prep_matmul"), sem("prep_evacuated")
        s_wgen, s_wev = sem("adapters_made"), sem("adapters_copied")
        s_normed = sem("conditioning_normed")
        s_hid0 = sem("adapter_hidden_ready")
        x_landed = [sem(f"x_landed{p}") for p in range(2)]
        y_stored = [sem(f"y_stored{p}") for p in range(2)]
        x_turned, x_copied = sem("x_turned"), sem("x_copied")
        y_turned, y_copied = sem("y_turned"), sem("y_copied")
        u_made, u_masked = sem("u_made"), sem("u_masked")
        v_made, v_masked = sem("v_made"), sem("v_masked")
        mid_made, hid_made = sem("mid_made"), sem("hid_made")
        mlp_made, z_made = sem("mlp_made"), sem("z_made")
        y_made = sem("y_made")
        gate_in, gate_out = sem("gate_in"), sem("gate_out")
        pre_made = sem("pre_made")
        hi_made, h_made, lo_made = sem("hi_made"), sem("h_made"), sem("lo_made")
        leaked = sem("leaked")

        def wait(eng, s, value):
            if not isinstance(value, int) or value > 0:
                eng.wait_ge(s, value)

        def landed(n, p):
            return 8 * TILES * (n - p) + 16 * TILES

        def each_block(eng, body, peeled=2):
            for n in (0, 1):
                body(n, n, 0, n + 2 < NBLK, True, n >= 1)
            with eng.Fori(1, (NBLK - peeled) // 2) as i:
                for p in range(2):
                    body(2 * i + p, p, i, True, True, True)
            for n in range(NBLK - peeled, NBLK):
                body(n, n % 2, n // 2, n + 2 < NBLK, n + 1 < NBLK, True)

        block = ctx.enter_context(nc.Block())

        @block.sync
        def _(sp):
            def load_x(n, p):
                for q in range(TILES):
                    sp.dma_start(x_nat[:, p, q, :],
                                 x[q * TILE_B:(q + 1) * TILE_B, bass.ds(n * TB, TB), :]
                                 ).then_inc(x_landed[p], 16)

            def store_y(n, p, half):
                for q in (2 * half, 2 * half + 1):
                    sp.dma_start(out[q * TILE_B:(q + 1) * TILE_B, bass.ds(n * TB, TB), :],
                                 y_nat[:, p, q, :]).then_inc(y_stored[p], 16)

            sp.dma_start(cond_sb[:, :], cond).then_inc(s_x0, 16)
            for i, v in enumerate((gamma, beta, bias1, alpha)):
                sp.dma_start(cols[:, i, :], v.rearrange("(c p) -> p c", p=P),
                             allow_slow_non_contiguous=True).then_inc(s_small, 16)
            sp.wait_ge(s_zero, 1)
            for i in range(3):
                sp.dma_start(b_rows[32 * i:32 * i + 1, :], b.rearrange("(a d) -> a d", a=1)).then_inc(s_small, 16)
            sp.dma_start(w1[:, :, :], W1.rearrange("(c p) n -> p c n", p=P)).then_inc(s_w1, 16)
            w2_v = W2.rearrange("(c p) (q n) -> p c q n", p=P, q=4)
            for j in range(4):
                for c in range(C):
                    sp.dma_start(w2[:, c, :, j * 512:(j + 1) * 512],
                                 w2_v[:, c, :, j * 512:(j + 1) * 512]).then_inc(s_w2[j], 16)
                if j == 1:
                    load_x(0, 0)
            load_x(1, 1)

            def body(n, p, i, front, mid, back):
                if not isinstance(n, int) or n + 3 < NBLK:
                    sp.wait_ge(x_turned, 2 * (n + 2))
                    load_x(n + 3, 1 - p)
                if back:
                    for half in range(2):
                        wait(sp, y_copied, 4 * (n - 1) + 2 * half + 2)
                        store_y(n - 1, 1 - p, half)

            sp.wait_ge(x_turned, 2)
            load_x(2, 0)
            each_block(sp, body, peeled=4)
            for half in range(2):
                sp.wait_ge(y_copied, 4 * (NBLK - 1) + 2 * half + 2)
                store_y(NBLK - 1, (NBLK - 1) % 2, half)
            for p in range(2):
                sp.wait_ge(y_stored[p], 16 * TILES * NBLK // 2)

        @block.gpsimd
        def _(pool):
            for c in range(C):
                pool.dma_start(w_nat[:, c, :], W[c * P:(c + 1) * P, :]).then_inc(s_w, 16)
            pool.dma_start(down[:, :, :], base_down.rearrange("(c p) n -> p c n", p=P)).then_inc(s_base, 16)
            pool.dma_start(up_nat[:, :, :], base_up.rearrange("(c p) n -> p c n", p=P)).then_inc(s_base, 16)
            bias2_v = bias2.rearrange("(q o n) -> q o n", q=4, o=1)
            for q in range(4):
                pool.dma_start(bias2_sb[q * B:(q + 1) * B, :],
                               bias2_v[q].broadcast_to([B, D * R])).then_inc(s_bias2, 16)
            pool.memset(ident[:, :], 0.0).then_inc(s_ident, 1)
            pool.wait_ge(s_ident, 1)
            pool.affine_select(out=ident[:, :], in_=ident[:, :], compare_op=ALU.not_equal, fill=1.0,
                               base=0, pattern=[[-1, P]], channel_multiplier=1).then_inc(s_ident, 1)
            pool.memset(mask[:, :, :], 1.0).then_inc(s_mask, 1)
            pool.wait_ge(s_mask, 1)
            for rows in (slice(0, P // 2), slice(P // 2, P)):
                pool.affine_select(out=mask[rows], in_=mask[rows], compare_op=ALU.is_ge, fill=0.0,
                                   base=0, pattern=[[-R, TILE_B], [0, TB]], channel_multiplier=1).then_inc(s_mask, 1)
            pool.wait_ge(s_mask, 3)
            for rows in (slice(0, P // 2), slice(P // 2, P)):
                pool.affine_select(out=mask[rows], in_=mask[rows], compare_op=ALU.is_ge, fill=0.0,
                                   base=R - 1, pattern=[[R, TILE_B], [0, TB]], channel_multiplier=-1).then_inc(s_mask, 1)

        @block.tensor
        def _(pe):
            def turn_x(n, p, half):
                if half == 0:
                    pe.wait_ge(x_landed[p], landed(n, p))
                    wait(pe, x_copied, 4 * n)
                    wait(pe, y_copied, 4 * (n - 3))
                else:
                    pe.wait_ge(x_copied, 4 * n + 2)
                for c in range(C):
                    for q in range(2):
                        mm = pe.transpose(turn[:, (2 * c + q) * P:(2 * c + q + 1) * P],
                                          x_nat[:, p, 2 * half + q, c * P:(c + 1) * P], ident[:, :])
                mm.then_inc(x_turned, 1)

            def turn_y(n, p, half):
                pe.wait_ge(y_made, 4 * n + 2 * half + 2)
                if half == 0:
                    pe.wait_ge(x_copied, 4 * min(n + 4, NBLK) if isinstance(n, int) else 4 * (n + 4))
                else:
                    pe.wait_ge(y_copied, 4 * n + 2)
                for q in range(2):
                    for c in range(C):
                        t0 = (2 * half + q) * P
                        mm = pe.transpose(turn[:, (2 * q + c) * P:(2 * q + c + 1) * P],
                                          yT[:, p, c, t0:t0 + P], ident[:, :])
                mm.then_inc(y_turned, 1)

            def project(q, src, g, made):
                for k in range(C):
                    for j in range(2):
                        t0 = (2 * g + j) * P
                        mm = pe.matmul(rank_ps[j * P // 2:(j + 1) * P // 2, g * P:(g + 1) * P],
                                       adapt[:, q, k, g, j * TILE_B:(j + 1) * TILE_B, :]
                                       .rearrange("p b r -> p (b r)"),
                                       src[:, k, t0:t0 + P], start=(k == 0), stop=(k == C - 1))
                if g == G - 1:
                    mm.then_inc(made, 1)

            def project_x(n, p, g):
                if g == 0:
                    pe.wait_ge(x_copied, 4 * (n + 1))
                    wait(pe, v_masked, 4 * n)
                project(2, xT[:, p, :, :], g, u_made)

            def project_hid(n, g):
                if g == 0:
                    pe.wait_ge(u_masked, 4 * (n + 1))
                    pe.wait_ge(hid_made, 4 * (n + 1))
                project(1, hid[:, :, :], g, v_made)

            def base(weights, src, m, k, halves):
                if len(halves) == 2:
                    pe.matmul(mlp[m][:, :], weights[:, k, m * P:(m + 1) * P], src[:, k, :],
                              start=(k == 0), stop=False, skip_group_check=True)
                else:
                    c0 = halves[0] * HALF
                    pe.matmul(mlp[m][:, c0:c0 + HALF], weights[:, k, m * P:(m + 1) * P],
                              src[:, k, c0:c0 + HALF], start=(k == 0 and c0 == 0), stop=False,
                              skip_group_check=True)

            def down_base(n, p, m, k, halves=(0, 1)):
                if k == 0 and 0 in halves:
                    wait(pe, z_made, 4 * (n - 1) + 2 * (m + 1))
                base(down, xT[:, p, :, :], m, k, halves)

            def down_adapter(n, m):
                pe.wait_ge(u_masked, 4 * (n + 1))
                for g in range(G):
                    mm = pe.matmul(mlp[m][:, g * HALF:(g + 1) * HALF], b2T[:, g, m * P:(m + 1) * P],
                                   u_sb[:, g, :, :].rearrange("p j t -> p (j t)"), start=False, stop=(g == G - 1), skip_group_check=True)
                mm.then_inc(mid_made, 1)

            def up_base(n, m, k, halves=(0, 1)):
                base(upT, hid[:, :, :], m, k, halves)

            def up_adapter(n, m):
                pe.wait_ge(v_masked, 4 * (n + 1))
                for g in range(G):
                    mm = pe.matmul(mlp[m][:, g * HALF:(g + 1) * HALF], a1T[:, g, m * P:(m + 1) * P],
                                   v_sb[:, g, :, :].rearrange("p j t -> p (j t)"), start=False, stop=(g == G - 1), skip_group_check=True)
                mm.then_inc(mlp_made, 1)

            def gate_bias(n, p, m):
                wait(pe, gate_out, 2 * TB * (n - 1))
                pe.matmul(pre_gate[p][m][:, :], b_part[:, m * P:(m + 1) * P], ones_bf[:, :],
                          start=True, stop=False, skip_group_check=True)

            def gate_z(n, p, m, k, halves=(0, 1)):
                pe.wait_ge(z_made, 4 * n + 2 * (k + 1))
                s0, s1 = halves[0] * TB // 2, (halves[-1] + 1) * TB // 2
                pe.matmul(pre_gate[p][m][:, s0 * B:s1 * B], wT[:, C + k, m * P:(m + 1) * P],
                          zp[:, p, k, s0:s1, :, 1].rearrange("p s b -> p (s b)"),
                          start=False, stop=False, skip_group_check=True)

            def first_half(n, p):
                turn_x(n, p, 0)
                turn_x(n, p, 1)
                for g in range(G):
                    project_x(n, p, g)
                for m in range(C):
                    for k in range(C):
                        down_base(n, p, m, k)
                    down_adapter(n, m)

            def second_half(n, p):
                for g in range(G):
                    project_hid(n, g)
                for m in range(C):
                    for k in range(C):
                        up_base(n, m, k)
                    up_adapter(n, m)
                for m in range(C):
                    gate_bias(n, p, m)
                for k in range(C):
                    for m in range(C):
                        gate_z(n, p, m, k)

            def side_work(s, n, p, front, mid, back):
                q = 1 - p
                if front and s == 0:
                    turn_x(n + 2, p, 0)
                if mid and s == 0:
                    project_hid(n + 1, 0)
                if mid and s == 1:
                    project_hid(n + 1, 1)
                    up_base(n + 1, 0, 0, (0,))
                if mid and s == 2:
                    up_base(n + 1, 0, 0, (1,))
                    up_base(n + 1, 0, 1)
                if front and s == 3:
                    turn_x(n + 2, p, 1)
                if mid and s == 3:
                    up_base(n + 1, 1, 0)
                if mid and s == 4:
                    up_base(n + 1, 1, 1)
                    gate_bias(n + 1, q, 0)
                if mid and s == 5:
                    up_adapter(n + 1, 0)
                    gate_bias(n + 1, q, 1)
                if mid and s == 6:
                    up_adapter(n + 1, 1)
                if front and s == 7:
                    project_x(n + 2, p, 0)
                    project_x(n + 2, p, 1)
                if back and s == 8:
                    turn_y(n - 1, q, 0)
                if front and s == 8:
                    down_base(n + 2, p, 0, 0)
                if front and s == 9:
                    down_base(n + 2, p, 0, 1)
                if front and s == 10:
                    down_adapter(n + 2, 0)
                    down_base(n + 2, p, 1, 0, (0,))
                if back and s == 11:
                    turn_y(n - 1, q, 1)
                if front and s == 11:
                    down_base(n + 2, p, 1, 0, (1,))
                    down_base(n + 2, p, 1, 1, (0,))
                if front and s == 12:
                    down_base(n + 2, p, 1, 1, (1,))
                    down_adapter(n + 2, 1)
                if mid and s == 13:
                    gate_z(n + 1, q, 0, 0)
                    gate_z(n + 1, q, 1, 0, (0,))
                if mid and s == 14:
                    gate_z(n + 1, q, 1, 0, (1,))
                    gate_z(n + 1, q, 0, 1, (0,))
                if mid and s == 15:
                    gate_z(n + 1, q, 0, 1, (1,))
                    gate_z(n + 1, q, 1, 1)

            def step(n, p, s):
                if not (isinstance(n, int) and n == 0 and s == 0):
                    done = 2 * (TB * n + s) - 2
                    for k in range(C):
                        pe.wait_ge(hi_made, done + k + 1)
                        for m in range(C):
                            for w in range(3):
                                pe.matmul(pre_gate[p][m][:, s * B:(s + 1) * B],
                                          wh_part[:, w, k, m * P:(m + 1) * P], h_hi[:, k, :],
                                          start=False, stop=False, skip_group_check=True)
                    for k in range(C):
                        pe.wait_ge(lo_made, done + k + 1)
                        for m in range(C):
                            for w in range(2):
                                mm = pe.matmul(pre_gate[p][m][:, s * B:(s + 1) * B],
                                               wh_part[:, w, k, m * P:(m + 1) * P], h_lo[:, k, :],
                                               start=False, stop=(k == C - 1 and w == 1),
                                               skip_group_check=True)
                            if k == C - 1:
                                mm.then_inc(gate_in, 1)

            def turned(dst, src, n_in=P):
                pe.transpose(dst, src, ident[0:n_in, 0:n_in]).then_inc(s_prep_pe, 1)

            pe.wait_ge(s_ident, 2)
            pe.wait_ge(s_normed, 1)
            for c in range(C):
                turned(turn[:, c * B:(c + 1) * B], cond_sb[:, c * P:(c + 1) * P], B)
            for c in range(C):
                turned(turn[:, (C + c) * B:(C + c + 1) * B], cond_n[:, c * P:(c + 1) * P], B)
            pe.wait_ge(s_w1, 16)
            pe.wait_ge(s_prep_ev, 1)
            for m in range(C):
                for k in range(C):
                    mm = pe.matmul(mlp[0][:, m * B:(m + 1) * B], w1[:, k, m * P:(m + 1) * P], cT[:, k, :],
                                   start=(k == 0), stop=(k == C - 1))
            mm.then_inc(s_prep_pe, 1)
            pe.wait_ge(s_w, 16 * C)
            for i in range(2 * C):
                bnk = (mlp[1], rank_ps)[i // 2]
                for j in range(C):
                    c0 = ((i % 2) * C + j) * P
                    mm = pe.transpose(bnk[:, c0:c0 + P], w_nat[:, j, i * P:(i + 1) * P], ident[:, :])
                if i % 2:
                    mm.then_inc(s_prep_pe, 1)
            pe.wait_ge(s_base, 32)
            pe.wait_ge(s_prep_ev, 1)
            for i in range(C):
                for j in range(C):
                    mm = pe.transpose(turn[:, (i * C + j) * P:(i * C + j + 1) * P],
                                      up_nat[:, j, i * P:(i + 1) * P], ident[:, :])
            mm.then_inc(s_prep_pe, 1)
            pe.wait_ge(s_hid0, 1)
            pe.wait_ge(s_prep_ev, 3)
            wbank = [mlp[0], mlp[1], rank_ps, pre_gate[0][0]]
            for j in range(4):
                pe.wait_ge(s_w2[j], 16 * C)
                for k in range(C):
                    for q in range(4):
                        mm = pe.matmul(wbank[j][q * B:(q + 1) * B, :], hidT0[:, k, :],
                                       w2[:, k, q, j * 512:(j + 1) * 512],
                                       start=(k == 0), stop=(k == C - 1), tile_position=(0, q * B))
                mm.then_inc(s_wgen, 1)
            tb = [turn, pre_gate[0][1], pre_gate[1][0], pre_gate[1][1]]
            pe.wait_ge(s_prep_ev, 4)
            for c in range(C):
                pe.wait_ge(s_wev, 2 * (c + 1))
                wv = w_all[:, :].rearrange("p (d r) -> p d r", r=R)
                for rh in range(2):
                    for r in range(4):
                        mm = pe.transpose(tb[2 * c + rh][:, r * P:(r + 1) * P],
                                          wv[:, c * P:(c + 1) * P, 4 * rh + r], ident[:, :])
                    mm.then_inc(s_wgen, 1)
            pe.wait_ge(s_wev, 4 + 16)
            for i, (q, bnk) in enumerate(((0, mlp[0]), (3, mlp[1]))):
                for g in range(G):
                    for c in range(C):
                        c0 = (g * C + c) * P
                        mm = pe.transpose(bnk[:, c0:c0 + P],
                                          adapt[:, q, c, g, :, :].rearrange("p b r -> p (b r)"), ident[:, :])
                mm.then_inc(s_wgen, 1)
            pe.wait_ge(s_wev, 4 + 16 + 2)
            first_half(0, 0)
            second_half(0, 0)
            for m in range(C):
                for k in range(C):
                    mm = pe.matmul(pre_gate[0][m][:, 0:B], wT[:, k, m * P:(m + 1) * P], condT[:, k, :],
                                   start=False, stop=(k == C - 1), skip_group_check=True)
                mm.then_inc(gate_in, 1)
            first_half(1, 1)

            def body(n, p, i, front, mid, back):
                for s in range(TB):
                    step(n, p, s)
                    side_work(s, n, p, front, mid, back)

            each_block(nc.tensor, body)
            turn_y(NBLK - 1, (NBLK - 1) % 2, 0)
            turn_y(NBLK - 1, (NBLK - 1) % 2, 1)

        @block.scalar
        def _(act):
            def copy_x(n, p, half, c):
                if c == 0:
                    act.wait_ge(x_turned, 2 * n + half + 1)
                    wait(act, z_made, 4 * (n - 1))
                act.activation(xT[:, p, c, half * HALF:(half + 1) * HALF],
                               turn[:, c * HALF:(c + 1) * HALF], ACT.Copy).then_inc(x_copied, 1)

            def copy_y(n, p, half, q):
                if q == 0:
                    act.wait_ge(y_turned, 2 * n + half + 1)
                    if half == 0:
                        wait(act, y_stored[p], 8 * TILES * (n - p))
                act.activation(y_nat[:, p, 2 * half + q, :], turn[:, q * D:(q + 1) * D],
                               ACT.Copy).then_inc(y_copied, 1)

            def gelu_piece(n, m, half):
                if half == 0:
                    act.wait_ge(mid_made, 2 * n + m + 1)
                c0 = half * HALF
                act.activation(hid[:, m, c0:c0 + HALF], mlp[m][:, c0:c0 + HALF],
                               ACT.Gelu).then_inc(hid_made, 1)

            def step(n, p, s):
                t2 = 2 * (TB * n + s)
                for c in range(C):
                    act.wait_ge(gate_in, t2 + c + 1)
                    act.activation(gl[:, c, :, 0], pre_gate[p][c][:, s * B:(s + 1) * B],
                                   ACT.Tanh, scale=0.5).then_inc(gate_out, 1)
                for c in range(C):
                    act.wait_ge(pre_made, t2 + c + 1)
                    act.activation(h_hi[:, c, :], pre[:, c, :, 1], ACT.Tanh).then_inc(hi_made, 1)
                    act.activation(h_all[:, p, c, s, :], pre[:, c, :, 1], ACT.Tanh).then_inc(h_made, 1)

            def side_work(s, n, p, front, mid, back):
                q = 1 - p
                if front and s in (1, 2):
                    copy_x(n + 2, p, 0, s - 1)
                if front and s in (4, 5):
                    copy_x(n + 2, p, 1, s - 4)
                if back and s in (9, 10):
                    copy_y(n - 1, q, 0, s - 9)
                if front and s in (11, 12):
                    gelu_piece(n + 2, 0, s - 11)
                if back and s in (12, 13):
                    copy_y(n - 1, q, 1, s - 12)
                if front and s in (13, 14):
                    gelu_piece(n + 2, 1, s - 13)

            act.wait_ge(s_dve, VARIANCE)
            act.activation(stat[:, 3:4], stat[:, 2:3], ACT.Sqrt).then_inc(s_act, 1)
            act.wait_ge(s_prep_pe, 5)
            for m in range(C):
                last = act.activation(hidT0[:, m, :], mlp[0][:, m * B:(m + 1) * B], ACT.Gelu,
                                      bias=cols[:, 2, m:m + 1])
            last.then_inc(s_hid0, 1)
            for n in range(2):
                for half in range(2):
                    for c in range(C):
                        copy_x(n, n, half, c)
                for m in range(C):
                    for half in range(2):
                        gelu_piece(n, m, half)

            def body(n, p, i, front, mid, back):
                wait(act, y_made, 4 * (n - 1))
                for s in range(TB):
                    step(n, p, s)
                    side_work(s, n, p, front, mid, back)

            each_block(nc.scalar, body)
            for half in range(2):
                for q in range(2):
                    copy_y(NBLK - 1, (NBLK - 1) % 2, half, q)

        @block.vector
        def _(dve):
            def mask_piece(n, made, masked, dst, g, j):
                if g == 0 and j == 0:
                    dve.wait_ge(made, n + 1)
                rows = slice(j * P // 2, (j + 1) * P // 2)
                dve.tensor_tensor(dst[rows, g, j, :], rank_ps[rows, g * P:(g + 1) * P],
                                  mask[rows, :, :].rearrange("p b s -> p (b s)"), ALU.mult).then_inc(masked, 1)

            def y_piece(n, p, g, c):
                if g == 0 and c == 0:
                    dve.wait_ge(h_made, 2 * TB * (n + 1))
                    wait(dve, y_turned, 2 * (n - 1))
                bs = slice(g * BG, (g + 1) * BG)
                dve.scalar_tensor_tensor(
                    yT[:, p, c, g * HALF:(g + 1) * HALF].rearrange("p (b s) -> p b s", b=BG),
                    zp[:, p, c, :, bs, 1].rearrange("p s b -> p b s"), 2.0,
                    h_all[:, p, c, :, bs].rearrange("p s b -> p b s"), ALU.mult, ALU.add).then_inc(y_made, 1)

            def z_piece(n, p, m, g):
                if g == 0:
                    dve.wait_ge(mlp_made, 2 * n + m + 1)
                    if m == 0:
                        wait(dve, y_made, 4 * (n - 1))
                c0 = g * HALF
                dve.scalar_tensor_tensor(
                    zp[:, p, m, :, g * BG:(g + 1) * BG, 1].rearrange("p s b -> p b s"),
                    mlp[m][:, c0:c0 + HALF].rearrange("p (b s) -> p b s", b=BG), 0.5,
                    xT[:, p, m, c0:c0 + HALF].rearrange("p (b s) -> p b s", b=BG),
                    ALU.mult, ALU.add).then_inc(z_made, 1)

            def leak_h(c, state, p, s):
                dve.scalar_tensor_tensor(gl[:, c, :, 1], state, leak_col[:, c:c + 1],
                                         zp[:, p, c, s, :, 1], ALU.mult, ALU.add).then_inc(leaked, 1)

            def step(n, p, s, front, mid, back):
                t = TB * n + s
                for c in range(C):
                    dve.wait_ge(gate_out, 2 * t + c + 1)
                    dve.wait_ge(leaked, 2 * t + c + 1)
                    dve.tensor_tensor_scan(pre[:, c, :, :].rearrange("p b j -> p (b j)"),
                                           zp[:, p, c, s, :, :].rearrange("p b j -> p (b j)"),
                                           gl[:, c, :, :].rearrange("p b j -> p (b j)"),
                                           0.0, ALU.mult, ALU.add).then_inc(pre_made, 1)
                side_work(s, n, p, front, mid, back)
                for c in range(C):
                    dve.wait_ge(h_made, 2 * t + c + 1)
                    dve.tensor_tensor(h_lo[:, c, :], h_all[:, p, c, s, :], h_hi[:, c, :],
                                      ALU.subtract).then_inc(lo_made, 1)
                if not (isinstance(n, int) and t == T - 1):
                    if s == TB - 1:
                        dve.wait_ge(z_made, 4 * (n + 2))
                    for c in range(C):
                        leak_h(c, h_all[:, p, c, s, :], *((p, s + 1) if s < TB - 1 else (1 - p, 0)))

            def side_work(s, n, p, front, mid, back):
                q = 1 - p
                if back and s in (0, 1):
                    y_piece(n - 1, q, 0, s)
                if mid and s in (2, 3):
                    for j in range(2):
                        mask_piece(n + 1, v_made, v_masked, v_sb, s - 2, j)
                if back and s in (4, 5):
                    y_piece(n - 1, q, 1, s - 4)
                if mid and s in (6, 7):
                    z_piece(n + 1, q, 0, s - 6)
                if mid and s in (8, 9):
                    z_piece(n + 1, q, 1, s - 8)

            def late_side_work(s, n, p, front):
                if front and s in (8, 9):
                    for j in range(2):
                        mask_piece(n + 2, u_made, u_masked, u_sb, s - 8, j)

            chain = [0]

            def link(ins):
                chain[0] += 1
                ins.then_inc(s_dve, 1)
                dve.wait_ge(s_dve, chain[0])

            dve.memset(b_rows[:, :], 0.0).then_inc(s_zero, 1)
            dve.wait_ge(s_x0, 16)
            link(dve.tensor_reduce(stat[:, 0:1], cond_sb[:, :], AX.X, ALU.add))
            link(dve.tensor_scalar(stat[:, 1:2], stat[:, 0:1], 1.0 / D, None, ALU.mult))
            link(dve.tensor_scalar(cond_n[:, :], cond_sb[:, :], stat[:, 1:2], None, ALU.subtract))
            link(dve.tensor_tensor(cond_sq[:, :], cond_n[:, :], cond_n[:, :], ALU.mult))
            link(dve.tensor_reduce(stat[:, 5:6], cond_sq[:, :], AX.X, ALU.add))
            link(dve.tensor_scalar(stat[:, 2:3], stat[:, 5:6], 1.0 / D, EPS, ALU.mult, ALU.add))
            dve.wait_ge(s_act, 1)
            link(dve.reciprocal(stat[:, 4:5], stat[:, 3:4]))
            dve.tensor_scalar(cond_n[:, :], cond_n[:, :], stat[:, 4:5], None, ALU.mult).then_inc(s_normed, 1)
            dve.wait_ge(s_small, 16 * 7)
            dve.wait_ge(s_prep_pe, 4)
            dve.tensor_copy(condT[:, :, :].rearrange("p c b -> p (c b)"), turn[:, 0:C * B])
            for c in range(C):
                last = dve.tensor_scalar(cT[:, c, :], turn[:, (C + c) * B:(C + c + 1) * B],
                                         cols[:, 0, c:c + 1], cols[:, 1, c:c + 1], ALU.mult, ALU.add)
            last.then_inc(s_prep_ev, 1)
            link(dve.memset(ones_bf[:, :], 1.0))
            link(dve.memset(u_sb[:, :, :, :].rearrange("p g j t -> p (g j t)"), 0.0))
            link(dve.memset(v_sb[:, :, :, :].rearrange("p g j t -> p (g j t)"), 0.0))
            link(dve.memset(zp[:, :, :, :, :, :].rearrange("p a c s b j -> p (a c s b j)"), 0.0))
            link(dve.tensor_scalar(leak_col[:, :], cols[:, 3, :], -1.0, 1.0, ALU.mult, ALU.add))
            dve.wait_ge(s_prep_pe, 7)
            dve.tensor_copy(wT[:, 0:C, :].rearrange("p c n -> p (c n)"), mlp[1][:, :]).then_inc(s_prep_ev, 1)
            dve.tensor_scalar(wT[:, C:2 * C, :].rearrange("p c n -> p (c n)"), rank_ps[:, :], 2.0, None,
                              ALU.mult).then_inc(s_prep_ev, 1)
            dve.wait_ge(s_prep_pe, 8)
            dve.tensor_copy(upT[:, :, :].rearrange("p c n -> p (c n)"), turn[:, :]).then_inc(s_prep_ev, 1)
            dve.wait_ge(s_prep_ev, 2)
            link(dve.tensor_copy(wh_part[:, 0, :, :], wT[:, 0:C, :]))
            link(dve.tensor_tensor(wh_rest[:, :, :], wT[:, 0:C, :], wh_part[:, 0, :, :], ALU.subtract))
            link(dve.tensor_copy(wh_part[:, 1, :, :], wh_rest[:, :, :]))
            link(dve.tensor_tensor(wh_part[:, 2, :, :], wh_rest[:, :, :], wh_part[:, 1, :, :], ALU.subtract))
            link(dve.memset(b_part[:, :], 0.0))
            link(dve.tensor_copy(b_hi[:, :], b_rows[:, :]))
            link(dve.tensor_tensor(b_rest[:, :], b_rows[:, :], b_hi[:, :], ALU.subtract))
            link(dve.tensor_copy(b_mid[:, :], b_rest[:, :]))
            link(dve.tensor_copy(b_part[0:1, :], b_hi[0:1, :]))
            link(dve.tensor_copy(b_part[32:33, :], b_mid[32:33, :]))
            link(dve.tensor_tensor(b_part[64:65, :], b_rest[64:65, :], b_mid[64:65, :], ALU.subtract))
            dve.wait_ge(s_bias2, 16 * 4)
            wbank = [mlp[0], mlp[1], rank_ps, pre_gate[0][0]]
            for j in range(4):
                dve.wait_ge(s_wgen, j + 1)
                dve.tensor_tensor(w_all[:, j * 512:(j + 1) * 512], wbank[j][:, :],
                                  bias2_sb[:, j * 512:(j + 1) * 512], ALU.add).then_inc(s_wev, 1)
            tb = [turn, pre_gate[0][1], pre_gate[1][0], pre_gate[1][1]]
            for c in range(C):
                for rh in range(2):
                    dve.wait_ge(s_wgen, 5 + 2 * c + rh)
                    for q in range(4):
                        src = tb[2 * c + rh][:, :].rearrange("p (r q g b) -> p q r g b", r=4, q=4, g=G)[:, q]
                        dst = adapt[:, q, c, :, :, 4 * rh:4 * rh + 4].rearrange("p g b r -> p r g b")
                        dve.tensor_copy(dst, src).then_inc(s_wev, 1)
            for i, (dst, bnk) in enumerate(((a1T, mlp[0]), (b2T, mlp[1]))):
                dve.wait_ge(s_wgen, 9 + i)
                dve.tensor_copy(dst[:, :, :].rearrange("p g n -> p (g n)"), bnk[:, :]).then_inc(s_wev, 1)
            dve.wait_ge(s_mask, 5)
            for n in range(2):
                for g in range(G):
                    for j in range(2):
                        mask_piece(n, u_made, u_masked, u_sb, g, j)
                if n == 0:
                    for g in range(G):
                        for j in range(2):
                            mask_piece(n, v_made, v_masked, v_sb, g, j)
                    for m in range(C):
                        for g in range(G):
                            z_piece(n, n, m, g)
                    dve.wait_ge(z_made, 4)
                    for c in range(C):
                        leak_h(c, condT[:, c, :], 0, 0)

            def body(n, p, i, front, mid, back):
                for s in range(TB):
                    step(n, p, s, front, mid, back)
                    late_side_work(s, n, p, front)

            each_block(nc.vector, body)
            for g in range(G):
                for c in range(C):
                    y_piece(NBLK - 1, (NBLK - 1) % 2, g, c)


_INS = ["x", "cond_1024", "L0_cond_base_up", "L0_cond_base_down", "L0_cond_ln_gamma", "L0_cond_ln_beta",
        "L0_cond_W1", "L0_cond_bias1", "L0_cond_W2", "L0_cond_bias2", "L1_cond_W", "L1_cond_b",
        "L1_cond_alpha"]


def kernel(**inputs):
    import numpy as np
    import concourse.bacc as bacc
    from concourse.bass_utils import run_bass_kernel_spmd

    nc = bacc.Bacc("TRN2", target_bir_lowering=False, num_devices=1)
    arrays, args = {}, []
    for name in _INS:
        a = np.ascontiguousarray(inputs[name])
        arrays[f"in_{name}"] = a
        args.append(nc.dram_tensor(f"in_{name}", a.shape, mybir.dt.from_np(a.dtype), kind="ExternalInput").ap())
    shape = inputs["x"].shape
    args.append(nc.dram_tensor("out_0", shape, F32, kind="ExternalOutput").ap())
    build(nc, *args)
    r = run_bass_kernel_spmd(nc, [arrays], core_ids=[0])
    return r.results[0]["out_0"]
```

```python
from contextlib import ExitStack

import concourse.bass as bass
from concourse import mybir

F32 = mybir.dt.float32
BF16 = mybir.dt.bfloat16
F16 = mybir.dt.float16
F32R = mybir.dt.float32r
ACT = mybir.ActivationFunctionType
ALU = mybir.AluOpType
AX = mybir.AxisListType

P = 128
EPS = 1e-5
GATE_BESIDE = {9: ((0, 1, "lh0"),), 10: ((0, 1, "lh1"),), 11: ((1, 1, "lh0"),), 12: ((1, 1, "lh1"),),
               13: ((0, 1, "hl0"),), 14: ((0, 1, "hl1"), (1, 1, "hl"), (0, 0, "hh")),
               15: ((0, 0, "lh"), (0, 0, "hl"), (1, 0, "hh"), (1, 0, "lh"), (1, 0, "hl0"))}
GATE_ALONE = {9: ((0, 1, "lh"), (1, 1, "lh")), 10: ((0, 0, "hh"), (1, 0, "hh")),
              11: ((0, 0, "lh"), (1, 0, "lh")), 12: ((0, 1, "hl"), (1, 1, "hl")),
              13: ((0, 0, "hl"),), 14: ((1, 0, "hl"),)}
WARM_UP = 20
VARIANCE = 6


def build(nc, x, cond, base_up, base_down, gamma, beta, W1, bias1, W2, bias2, W, b, alpha, out):
    B, T, D = x.shape
    C = D // P
    R = W2.shape[1] // (4 * D)
    TB = 512 // B
    NBLK = T // TB
    TOK = B * TB
    BG = P // R
    G = B // BG
    HALF = TOK // 2
    TILE_B = P // TB
    TILES = TOK // P
    EARLY = 3 * TB // 4 - 1
    assert C == 2 and G == 2 and TILES == 4 and NBLK % 2 == 0 and NBLK >= 6

    with ExitStack() as ctx:
        def sb(name, shape, dt=F32):
            return ctx.enter_context(nc.sbuf_tensor(name, shape, dt))

        def bank(name):
            return ctx.enter_context(nc.psum_tensor(name, [P, 512], F32))

        def sem(name):
            return ctx.enter_context(nc.semaphore(name))

        pre_gate = [[bank(f"pre_gate{p}{m}") for m in range(C)] for p in range(2)]
        mlp = [bank(f"mlp{m}") for m in range(C)]
        spare = bank("spare")
        turn = bank("turn")

        ident = sb("ident", [P, P])
        mask = sb("mask", [P, TILE_B, TB])
        w_nat = sb("w_nat", [P, C, 2 * D])
        wT = sb("wT", [P, 2 * C, D])
        wh_rest = sb("wh_rest", [P, C, D])
        wh_part = sb("wh_part", [P, 3, C, D], BF16)
        down = sb("down", [P, C, D])
        up_nat = sb("up_nat", [P, C, D])
        upT = sb("upT", [P, C, D])
        down_hi, down_lo = (sb(f"down_{w}", [P, C, D], F32R) for w in ("hi", "lo"))
        up_hi, up_lo = (sb(f"up_{w}", [P, C, D], F32R) for w in ("hi", "lo"))
        wz_hi, wz_lo = (sb(f"wz_{w}", [P, C, D], F32R) for w in ("hi", "lo"))
        ones_bf = sb("ones_bf", [P, TOK], BF16)
        b_rows = sb("b_rows", [P, D])
        b_rest = sb("b_rest", [P, D])
        b_hi = sb("b_hi", [P, D], BF16)
        b_mid = sb("b_mid", [P, D], BF16)
        b_part = sb("b_part", [P, D], BF16)
        w1 = sb("w1", [P, C, D])
        w2 = sb("w2", [P, 2, 2, C, 4, P * R // 2])
        biasT = sb("biasT", [P, 4, C, R])
        w_all = sb("w_all", [P, 2, P * R])
        adapt = sb("adapt", [P, 4, C, B, R])
        a1T = sb("a1T", [P, G, D])
        b2T = sb("b2T", [P, G, D])
        cond_sb = sb("cond_sb", [B, D])
        cond_sq = sb("cond_sq", [B, D])
        cond_n = sb("cond_n", [B, D])
        stat = sb("stat", [B, 8])
        cols = sb("cols", [P, 4, C])
        leak_col = sb("leak_col", [P, C])
        condT = sb("condT", [P, C, B])
        cT = sb("cT", [P, C, B])
        hidT0 = sb("hidT0", [P, C, B])
        x_nat = sb("x_nat", [P, 2, TILES, D])
        xT = sb("xT", [P, 2, C, TOK])
        u_sb = sb("u_sb", [P, G, 2, P])
        v_sb = sb("v_sb", [P, G, 2, P])
        x_hi, x_lo = (sb(f"x_{w}", [P, C, TOK], F32R) for w in ("hi", "lo"))
        hid = sb("hid", [P, C, TOK])
        hid_hi, hid_lo = (sb(f"hid_{w}", [P, C, TOK], F32R) for w in ("hi", "lo"))
        z_hi, z_lo = (sb(f"z_{w}", [P, C, TB, B], F32R) for w in ("hi", "lo"))
        zp = sb("zp", [P, 2, C, TB, B, 2])
        h_all = sb("h_all", [P, 2, C, TB, B])
        yT = w2[:, 0, 0, 0, :, :].rearrange("p g n -> p (g n)").rearrange("p (a c t) -> p a c t", a=2, c=C)
        y_nat = w2[:, 0, 0, 1, :, :].rearrange("p g n -> p (g n)").rearrange("p (a q d) -> p a q d", a=2, q=TILES)
        gl = sb("gl", [P, C, B, 2])
        pre = [sb("pre0", [P, B, 2]), spare[:, 0:2 * B].rearrange("p (b j) -> p b j", j=2)]
        h_hi = sb("h_hi", [P, C, B], F16)
        h_lo = sb("h_lo", [P, C, B], F16)

        s_small, s_b, s_w, s_base, s_w1, s_bias2, s_x0 = (sem(n) for n in (
            "small_landed", "b_landed", "w_landed", "base_landed", "w1_landed", "bias2_landed", "cond_landed"))
        s_w2 = [[sem(f"w2_landed{j}{k}") for k in range(C)] for j in range(4)]
        s_zero = sem("zeroed")
        s_parts = sem("weight_parts_ready")
        s_ident, s_mask = sem("ident_ready"), sem("mask_ready")
        s_dve, s_act = sem("dve_chain"), sem("act_chain")
        s_prep_pe, s_prep_ev = sem("prep_matmul"), sem("prep_evacuated")
        s_wgen, s_wcopy = sem("adapters_made"), sem("adapters_copied")
        s_wturn, s_adapt = sem("adapters_turned"), sem("adapters_ready")
        s_rows_ps, s_rows = sem("adapter_rows_turned"), sem("adapter_rows_ready")
        s_pairs = sem("pairs_cleared")
        s_normed, s_cond = sem("conditioning_normed"), sem("conditioning_ready")
        s_hid0 = sem("adapter_hidden_ready")
        x_landed = [sem(f"x_landed{p}") for p in range(2)]
        y_stored = [sem(f"y_stored{p}") for p in range(2)]
        x_turned, x_copied = sem("x_turned"), sem("x_copied")
        y_turned, y_copied = sem("y_turned"), sem("y_copied")
        u_made, u_masked = sem("u_made"), sem("u_masked")
        v_made, v_masked = sem("v_made"), sem("v_masked")
        mid_made, hid_made = sem("mid_made"), sem("hid_made")
        mlp_made, z_made = sem("mlp_made"), sem("z_made")
        y_made = sem("y_made")
        last_copied = sem("last_copied")
        x_hi_made, x_lo_made = sem("x_hi_made"), sem("x_lo_made")
        hid_hi_made, hid_lo_made = sem("hid_hi_made"), sem("hid_lo_made")
        z_hi_made, z_lo_made = sem("z_hi_made"), sem("z_lo_made")
        gate_in, gate_out = sem("gate_in"), sem("gate_out")
        pre_made = sem("pre_made")
        hi_made, h_made, lo_made = sem("hi_made"), sem("h_made"), sem("lo_made")
        leaked = sem("leaked")

        def wait(eng, s, value):
            if not isinstance(value, int) or value > 0:
                eng.wait_ge(s, value)

        def landed(n, p):
            return 8 * TILES * (n - p) + 16 * TILES

        def each_block(eng, body, peeled=2):
            for n in (0, 1):
                body(n, n, 0, n + 2 < NBLK, True, n >= 1)
            with eng.Fori(1, (NBLK - peeled) // 2) as i:
                for p in range(2):
                    body(2 * i + p, p, i, True, True, True)
            for n in range(NBLK - peeled, NBLK):
                body(n, n % 2, n // 2, n + 2 < NBLK, n + 1 < NBLK, True)

        block = ctx.enter_context(nc.Block())

        @block.sync
        def _(sp):
            def load_x(n, p):
                for q in range(TILES):
                    sp.dma_start(x_nat[:, p, q, :],
                                 x[q * TILE_B:(q + 1) * TILE_B, bass.ds(n * TB, TB), :]
                                 ).then_inc(x_landed[p], 16)

            def store_y(n, p, half):
                for q in (2 * half, 2 * half + 1):
                    sp.dma_start(out[q * TILE_B:(q + 1) * TILE_B, bass.ds(n * TB, TB), :],
                                 y_nat[:, p, q, :]).then_inc(y_stored[p], 16)

            def load_w2(stage, piece):
                view = W2.rearrange("(k p) (t g j n) -> k t j p g n", p=P, t=2, g=4, j=2)
                for k in range(C):
                    sp.dma_start(w2[:, stage, piece, k, :, :], view[k, 1 - stage, piece]
                                 ).then_inc(s_w2[2 * stage + piece][k], 16)

            sp.dma_start(cond_sb[:, :], cond).then_inc(s_x0, 16)
            load_x(0, 0)
            for i, v in enumerate((gamma, beta, bias1, alpha)):
                sp.dma_start(cols[:, i, :], v.rearrange("(c p) -> p c", p=P),
                             allow_slow_non_contiguous=True).then_inc(s_small, 16)
            load_x(1, 1)
            load_w2(0, 0)
            load_w2(0, 1)
            load_w2(1, 0)
            load_w2(1, 1)

            def body(n, p, i, front, mid, back):
                if not isinstance(n, int) or n + 3 < NBLK:
                    sp.wait_ge(x_turned, 2 * (n + 2))
                    load_x(n + 3, 1 - p)
                if back:
                    for half in range(2):
                        wait(sp, y_copied, 4 * (n - 1) + 2 * half + 2)
                        store_y(n - 1, 1 - p, half)

            sp.wait_ge(x_turned, 2)
            load_x(2, 0)
            each_block(sp, body, peeled=4)
            sp.wait_ge(y_copied, 4 * (NBLK - 1) + 2)
            store_y(NBLK - 1, (NBLK - 1) % 2, 0)
            sp.wait_ge(last_copied, 2)
            store_y(NBLK - 1, (NBLK - 1) % 2, 1)
            for p in range(2):
                sp.wait_ge(y_stored[p], 16 * TILES * NBLK // 2)

        @block.gpsimd
        def _(pool):
            pool.memset(ident[:, :], 0.0).then_inc(s_ident, 1)
            pool.wait_ge(s_ident, 1)
            pool.affine_select(out=ident[:, :], in_=ident[:, :], compare_op=ALU.not_equal, fill=1.0,
                               base=0, pattern=[[-1, P]], channel_multiplier=1).then_inc(s_ident, 1)
            pool.dma_start(w_nat[:, :, :], W.rearrange("(c p) n -> p c n", p=P)).then_inc(s_w, 16)
            pool.dma_start(up_nat[:, :, :], base_up.rearrange("(c p) n -> p c n", p=P)).then_inc(s_base, 16)
            pool.dma_start(down[:, :, :], base_down.rearrange("(c p) n -> p c n", p=P)).then_inc(s_base, 16)
            pool.dma_start(w1[:, :, :], W1.rearrange("(c p) n -> p c n", p=P)).then_inc(s_w1, 16)
            pool.memset(mask[:, :, :], 1.0).then_inc(s_mask, 1)
            pool.wait_ge(s_mask, 1)
            for rows in (slice(0, P // 2), slice(P // 2, P)):
                pool.affine_select(out=mask[rows], in_=mask[rows], compare_op=ALU.is_ge, fill=0.0,
                                   base=0, pattern=[[-R, TILE_B], [0, TB]], channel_multiplier=1).then_inc(s_mask, 1)
            pool.wait_ge(s_mask, 3)
            for rows in (slice(0, P // 2), slice(P // 2, P)):
                pool.affine_select(out=mask[rows], in_=mask[rows], compare_op=ALU.is_ge, fill=0.0,
                                   base=R - 1, pattern=[[R, TILE_B], [0, TB]], channel_multiplier=-1).then_inc(s_mask, 1)
            pool.wait_ge(s_mask, 5)
            pool.memset(zp[:, :, :, :, :, 0].rearrange("p a c s b -> p (a c s b)"), 0.0).then_inc(s_pairs, 1)

        @block.tensor
        def _(pe):
            def turn_x(n, p, half):
                if half == 0:
                    pe.wait_ge(x_landed[p], landed(n, p))
                    wait(pe, x_copied, 4 * n)
                    wait(pe, x_hi_made, 4 * (n - 2))
                    wait(pe, y_copied, 4 * (n - 3))
                else:
                    pe.wait_ge(x_copied, 4 * n + 2)
                    wait(pe, x_hi_made, 4 * (n - 2) + 2 if not isinstance(n, int) or n >= 2 else 0)
                for c in range(C):
                    for q in range(2):
                        mm = pe.transpose(turn[:, (2 * c + q) * P:(2 * c + q + 1) * P],
                                          x_nat[:, p, 2 * half + q, c * P:(c + 1) * P], ident[:, :])
                mm.then_inc(x_turned, 1)

            def turn_y(n, p, half, bnk=turn):
                pe.wait_ge(y_made, 4 * n + half + 3)
                if half == 0:
                    pe.wait_ge(x_copied, 4 * min(n + 4, NBLK) if isinstance(n, int) else 4 * (n + 4))
                    pe.wait_ge(x_hi_made, 4 * min(n + 2, NBLK - 2) if isinstance(n, int) else 4 * (n + 2))
                elif bnk is turn:
                    pe.wait_ge(y_copied, 4 * n + 2)
                for q in range(2):
                    for c in range(C):
                        t0 = (2 * half + q) * P
                        mm = pe.transpose(bnk[:, (2 * q + c) * P:(2 * q + c + 1) * P],
                                          yT[:, p, c, t0:t0 + P], ident[:, :])
                mm.then_inc(y_turned, 1)

            def project(q, src, g, made, bnk):
                for k in range(C):
                    for j in range(2):
                        t0, b0 = (2 * g + j) * P, (2 * g + j) * TILE_B
                        mm = pe.matmul(bnk[j * P // 2:(j + 1) * P // 2, g * P:(g + 1) * P],
                                       adapt[:, q, k, b0:b0 + TILE_B, :]
                                       .rearrange("p b r -> p (b r)"),
                                       src[:, k, t0:t0 + P], start=(k == 0), stop=(k == C - 1))
                if g == G - 1:
                    mm.then_inc(made, 1)

            def project_x(n, p, g, bnk=mlp[1]):
                if g == 0:
                    pe.wait_ge(x_copied, 4 * (n + 1))
                    if bnk is not spare:
                        pe.wait_ge(z_made, 4 * (n - 1) + 2)
                project(2, xT[:, p, :, :], g, u_made, bnk)

            def project_hid(n, g, bnk=mlp[0]):
                if g == 0:
                    pe.wait_ge(hid_made, 4 * (n + 1))
                    wait(pe, hid_hi_made, 4 * (n - 1) + 2 if bnk is not spare else 0)
                project(1, hid[:, :, :], g, v_made, bnk)

            def product(out_cols, weights, src, m, k, start=False, stop=False):
                return pe.matmul(out_cols, weights[:, k, m * P:(m + 1) * P], src, start=start, stop=stop,
                                 skip_group_check=True)

            def down_base_f32(p, m, k, bank):
                product(bank[:, :], down, xT[:, p, k, :], m, k, start=(k == 0))

            def up_base_f32(m, k):
                product(mlp[m][:, :], upT, hid[:, k, :], m, k, start=(k == 0))

            def parts_product(bank, w_hi, w_lo, src_hi, src_lo, m, k, part, opens):
                half = slice(0, TOK) if len(part) == 2 else slice(int(part[2]) * HALF, (int(part[2]) + 1) * HALF)
                product(bank[:, half], w_lo if part[:2] == "lh" else w_hi,
                        (src_lo if part[:2] == "hl" else src_hi)[:, half], m, k,
                        start=(opens and k == 0 and part in ("hh", "hh0")))

            def down_base(n, m, k, parts):
                for part in parts:
                    if part == "hh":
                        pe.wait_ge(x_hi_made, 4 * (n - 1))
                        if k == 0 and m == 0:
                            pe.wait_ge(z_made, 4 * n)
                        if k == 0 and m == 1:
                            pe.wait_ge(u_masked, 2 * (n + 1))
                    if part[:2] == "hl":
                        pe.wait_ge(x_lo_made, 4 * (n - 1))
                    parts_product(mlp[m], down_hi, down_lo, x_hi[:, k, :], x_lo[:, k, :], m, k, part, True)

            def up_base(n, m, k, parts):
                for part in parts:
                    if part == "hh" and k == 0:
                        pe.wait_ge(hid_hi_made, 4 * n)
                        if m == 0:
                            pe.wait_ge(v_masked, 2 * (n + 1))
                    if part[:2] == "hl":
                        pe.wait_ge(hid_lo_made, 4 * (n - 1) + 2 * (k + 1))
                    parts_product(mlp[m], up_hi, up_lo, hid_hi[:, k, :], hid_lo[:, k, :], m, k, part, True)

            def down_adapter(n, m, groups=(0, 1), banks=mlp):
                pe.wait_ge(u_masked, 2 * (n + 1))
                for g in groups:
                    mm = pe.matmul(banks[m][:, g * HALF:(g + 1) * HALF], b2T[:, g, m * P:(m + 1) * P],
                                   u_sb[:, g, :, :].rearrange("p j t -> p (j t)"), start=False, stop=(g == G - 1), skip_group_check=True)
                if G - 1 in groups:
                    mm.then_inc(mid_made, 1)

            def up_adapter(n, m, groups=(0, 1)):
                pe.wait_ge(v_masked, 2 * (n + 1))
                for g in groups:
                    mm = pe.matmul(mlp[m][:, g * HALF:(g + 1) * HALF], a1T[:, g, m * P:(m + 1) * P],
                                   v_sb[:, g, :, :].rearrange("p j t -> p (j t)"), start=False, stop=(g == G - 1), skip_group_check=True)
                if G - 1 in groups:
                    mm.then_inc(mlp_made, 1)

            def gate_bias(n, p, m):
                wait(pe, gate_out, 2 * TB * (n - 1))
                pe.matmul(pre_gate[p][m][:, :], b_part[:, m * P:(m + 1) * P], ones_bf[:, :],
                          start=True, stop=False, skip_group_check=True)

            def gate_z_f32(m, k, half, stop=False):
                pe.wait_ge(z_made, 4 - 2 * k)
                steps = slice(half * TB // 2, (half + 1) * TB // 2)
                return product(pre_gate[0][m][:, half * HALF:(half + 1) * HALF], wT[:, C:2 * C, :],
                               zp[:, 0, k, steps, :, 1].rearrange("p s b -> p (s b)"), m, k, stop=stop)

            def gate_z(n, p, m, k, parts):
                for part in parts:
                    if part[:2] == "hl":
                        pe.wait_ge(z_lo_made, 4 * n - 2 * k)
                    else:
                        pe.wait_ge(z_hi_made, 4 * n - 2 * k)
                    parts_product(pre_gate[p][m], wz_hi, wz_lo,
                                  z_hi[:, k, :, :].rearrange("p s b -> p (s b)"),
                                  z_lo[:, k, :, :].rearrange("p s b -> p (s b)"), m, k, part, False)

            def side_work(s, n, p, front, mid, back):
                q = 1 - p
                if front and s == 0:
                    turn_x(n + 2, p, 0)
                if mid and s == 0:
                    project_hid(n + 1, 0)
                if mid and s == 1:
                    project_hid(n + 1, 1)
                    up_base(n + 1, 1, 0, ("hh", "lh"))
                if mid and s == 2:
                    up_base(n + 1, 1, 0, ("hl",))
                    up_base(n + 1, 1, 1, ("hh", "lh"))
                    gate_bias(n + 1, q, 0)
                if back and mid and s == 2:
                    pe.wait_ge(gate_out, 2 * (TB * n + s) + 2)
                    gate_z(n, p, 1, 0, ("hl1",))
                if mid and s == 3:
                    up_base(n + 1, 1, 1, ("hl",))
                if front and s == 3:
                    turn_x(n + 2, p, 1)
                if mid and s == 3:
                    up_base(n + 1, 0, 0, ("hh", "lh0"))
                if mid and s == 4:
                    up_adapter(n + 1, 1)
                    up_base(n + 1, 0, 0, ("lh1",))
                if mid and s == 5:
                    up_base(n + 1, 0, 0, ("hl",))
                    up_base(n + 1, 0, 1, ("hh", "lh", "hl0"))
                    gate_bias(n + 1, q, 1)
                if mid and s == 6:
                    up_base(n + 1, 0, 1, ("hl1",))
                    up_adapter(n + 1, 0)
                if front and s == 7:
                    project_x(n + 2, p, 0)
                if back and s == 7:
                    turn_y(n - 1, q, 0)
                if front and s == 8:
                    project_x(n + 2, p, 1)
                if mid and s == 8:
                    gate_z(n + 1, q, 0, 1, ("hh",))
                    gate_z(n + 1, q, 1, 1, ("hh",))
                if front and s == 9:
                    down_base(n + 2, 0, 0, ("hh", "lh", "hl"))
                    down_base(n + 2, 0, 1, ("hh",))
                if front and s == 10:
                    down_base(n + 2, 0, 1, ("lh", "hl"))
                if back and s == 10:
                    turn_y(n - 1, q, 1)
                if front and s == 11:
                    down_base(n + 2, 1, 0, ("hh", "lh", "hl"))
                    down_base(n + 2, 1, 1, ("hh",))
                if front and s == 12:
                    down_adapter(n + 2, 0)
                if front and s == 13:
                    down_base(n + 2, 1, 1, ("lh", "hl"))
                    down_adapter(n + 2, 1, (0,))
                if front and s == 14:
                    down_adapter(n + 2, 1, (1,))
                if mid:
                    for m, k, part in (GATE_BESIDE if front else GATE_ALONE).get(s, ()):
                        gate_z(n + 1, q, m, k, (part,))
                if not back and s in (0, 1, 2, 3):
                    pe.wait_ge(gate_out, 2 * s + s % 2 + 1)
                    gate_z_f32(s % 2, s // 2, 1)

            def step(n, p, s):
                if not (isinstance(n, int) and n == 0 and s == 0):
                    done = 2 * (TB * n + s) - 2
                    for k in range(C):
                        pe.wait_ge(hi_made, done + k + 1)
                        for m in range(C):
                            for w in range(3):
                                pe.matmul(pre_gate[p][m][:, s * B:(s + 1) * B],
                                          wh_part[:, w, k, m * P:(m + 1) * P], h_hi[:, k, :],
                                          start=False, stop=False, skip_group_check=True)
                    for k in range(C):
                        pe.wait_ge(lo_made, done + k + 1)
                        for m in range(C):
                            for w in range(2):
                                mm = pe.matmul(pre_gate[p][m][:, s * B:(s + 1) * B],
                                               wh_part[:, w, k, m * P:(m + 1) * P], h_lo[:, k, :],
                                               start=False, stop=(k == C - 1 and w == 1),
                                               skip_group_check=True)
                            if k == C - 1:
                                mm.then_inc(gate_in, 1)

            def turned(dst, src, n_in=P):
                pe.transpose(dst, src, ident[0:n_in, 0:n_in]).then_inc(s_prep_pe, 1)

            pe.wait_ge(s_ident, 2)
            for _ in range(WARM_UP):
                pe.transpose(mlp[0][:, 0:P], ident[:, :], ident[:, :])
            pe.wait_ge(s_w, 16)
            for i in range(2 * C):
                for j in range(C):
                    c0 = ((i % 2) * C + j) * P
                    mm = pe.transpose(pre_gate[0][i // 2][:, c0:c0 + P],
                                      w_nat[:, j, i * P:(i + 1) * P], ident[:, :])
                if i % 2:
                    mm.then_inc(s_prep_pe, 1)
            pe.wait_ge(s_base, 32)
            for i in range(C):
                for j in range(C):
                    mm = pe.transpose(spare[:, (i * C + j) * P:(i * C + j + 1) * P],
                                      up_nat[:, j, i * P:(i + 1) * P], ident[:, :])
            mm.then_inc(s_prep_pe, 1)
            turn_x(0, 0, 0)
            pe.wait_ge(s_normed, 1)
            for c in range(C):
                turned(pre_gate[1][0][:, c * B:(c + 1) * B], cond_sb[:, c * P:(c + 1) * P], B)
            for c in range(C):
                turned(pre_gate[1][0][:, (C + c) * B:(C + c + 1) * B],
                       cond_n[:, c * P:(c + 1) * P], B)
            turn_x(0, 0, 1)
            pe.wait_ge(s_w1, 16)
            pe.wait_ge(s_cond, 1)
            for m in range(C):
                for k in range(C):
                    mm = pe.matmul(pre_gate[1][1][:, m * B:(m + 1) * B], w1[:, k, m * P:(m + 1) * P],
                                   cT[:, k, :], start=(k == 0), stop=(k == C - 1))
            mm.then_inc(s_prep_pe, 1)

            def make_adapters(stage, piece, chunks=range(C)):
                for k in chunks:
                    pe.wait_ge(s_w2[2 * stage + piece][k], 16)
                    for g in range(4):
                        mm = pe.matmul(pre_gate[0][piece][g * B:(g + 1) * B, :], hidT0[:, k, :],
                                       w2[:, stage, piece, k, g, :],
                                       start=(k == 0), stop=(k == C - 1), tile_position=(0, g * B))
                if C - 1 in chunks:
                    mm.then_inc(s_wgen, 1)

            def turn_adapters(stage, banks):
                pe.wait_ge(s_wcopy, 2 * (stage + 1))
                if stage == 1:
                    pe.wait_ge(u_masked, 4)
                wv = w_all[:, stage, :].rearrange("p (d r) -> p d r", r=R)
                for rh in range(2):
                    for r in range(4):
                        mm = pe.transpose(banks[rh][:, r * P:(r + 1) * P], wv[:, :, 4 * rh + r], ident[:, :])
                    mm.then_inc(s_wturn, 1)

            def turn_rows(stage, q, bnk):
                pe.wait_ge(s_adapt, 2 * (stage + 1))
                for g in range(G):
                    for c in range(C):
                        c0 = (g * C + c) * P
                        mm = pe.transpose(bnk[:, c0:c0 + P],
                                          adapt[:, q, c, g * BG:(g + 1) * BG, :].rearrange("p b r -> p (b r)"),
                                          ident[:, :])
                mm.then_inc(s_rows_ps, 1)

            pe.wait_ge(x_copied, 4)
            for m in range(C):
                for k in range(C):
                    down_base_f32(0, m, k, mlp[m])
            pe.wait_ge(s_prep_ev, 3)
            pe.wait_ge(s_hid0, 1)
            turn_x(1, 1, 0)
            make_adapters(0, 0)
            turn_x(1, 1, 1)
            pe.wait_ge(x_copied, 8)
            for k in range(C):
                down_base_f32(1, 0, k, pre_gate[1][0])
            make_adapters(0, 1)
            down_base_f32(1, 1, 0, pre_gate[1][1])
            turn_adapters(0, (turn, spare))
            down_base_f32(1, 1, 1, pre_gate[1][1])
            make_adapters(1, 0, (0,))
            turn_rows(0, 3, pre_gate[0][1])
            for g in range(G):
                project_x(0, 0, g, spare)
            make_adapters(1, 0, (1,))
            pe.wait_ge(s_rows, 1)
            for m in range(C):
                down_adapter(0, m)
            for g in range(G):
                project_x(1, 1, g, spare)
            make_adapters(1, 1)
            pe.wait_ge(hid_made, 4)
            for k in range(C):
                up_base_f32(0, k)
            turn_adapters(1, (turn, spare))
            for k in range(C):
                up_base_f32(1, k)
            pe.wait_ge(s_adapt, 4)
            for g in range(G):
                project_hid(0, g, spare)
            turn_rows(1, 0, pre_gate[0][1])
            for m in range(C):
                down_adapter(1, m, banks=pre_gate[1])
            pe.wait_ge(s_rows, 2)
            for m in (1, 0):
                up_adapter(0, m)
            for m in range(C):
                gate_bias(0, 0, m)
            for m in range(C):
                for k in range(C):
                    pe.matmul(pre_gate[0][m][:, 0:B], wT[:, k, m * P:(m + 1) * P], condT[:, k, :],
                              start=False, stop=False, skip_group_check=True)
            for k in (1, 0):
                for m in range(C):
                    mm = gate_z_f32(m, k, 0, stop=(k == 0))
                    if k == 0:
                        mm.then_inc(gate_in, 1)

            def body(n, p, i, front, mid, back):
                for s in range(TB):
                    step(n, p, s)
                    side_work(s, n, p, front, mid, back)

            pe.wait_ge(s_parts, 3)
            each_block(nc.tensor, body)
            turn_y(NBLK - 1, (NBLK - 1) % 2, 0)
            turn_y(NBLK - 1, (NBLK - 1) % 2, 1, mlp[0])

        @block.scalar
        def _(act):
            def copy_x(n, p, half, c):
                if c == 0:
                    act.wait_ge(x_turned, 2 * n + half + 1)
                    wait(act, z_made, 4 * (n - 1))
                act.activation(xT[:, p, c, half * HALF:(half + 1) * HALF],
                               turn[:, c * HALF:(c + 1) * HALF], ACT.Copy).then_inc(x_copied, 1)

            def copy_x_hi(n, half, c):
                if half == 0 and c == 0:
                    wait(act, mid_made, 2 * n if not isinstance(n, int) or n > 2 else 0)
                act.activation(x_hi[:, c, half * HALF:(half + 1) * HALF],
                               turn[:, c * HALF:(c + 1) * HALF], ACT.Copy).then_inc(x_hi_made, 1)

            def gelu_hi_piece(n, m, half, banks=mlp):
                c0 = half * HALF
                act.activation(hid_hi[:, m, c0:c0 + HALF], banks[m][:, c0:c0 + HALF],
                               ACT.Gelu).then_inc(hid_hi_made, 1)

            def z_hi_piece(n, p, m, g):
                act.wait_ge(z_made, 4 * n + 2 * (1 - m) + g + 1)
                bs = slice(g * BG, (g + 1) * BG)
                act.activation(z_hi[:, m, :, bs], zp[:, p, m, :, bs, 1], ACT.Copy).then_inc(z_hi_made, 1)

            def copy_y(n, p, half, q):
                if q == 0:
                    act.wait_ge(y_turned, 2 * n + half + 1)
                    if half == 0:
                        wait(act, y_stored[p], 8 * TILES * (n - p))
                act.activation(y_nat[:, p, 2 * half + q, :], turn[:, q * D:(q + 1) * D],
                               ACT.Copy).then_inc(y_copied, 1)

            def gelu_piece(n, m, half, banks=mlp):
                if half == 0:
                    act.wait_ge(mid_made, 2 * n + m + 1)
                c0 = half * HALF
                act.activation(hid[:, m, c0:c0 + HALF], banks[m][:, c0:c0 + HALF],
                               ACT.Gelu).then_inc(hid_made, 1)

            def step(n, p, s):
                t2 = 2 * (TB * n + s)
                for c in range(C):
                    act.wait_ge(gate_in, t2 + c + 1)
                    act.activation(gl[:, c, :, 0], pre_gate[p][c][:, s * B:(s + 1) * B],
                                   ACT.Tanh, scale=0.5).then_inc(gate_out, 1)
                for c in range(C):
                    act.wait_ge(pre_made, t2 + c + 1)
                    act.activation(h_hi[:, c, :], pre[c][:, :, 1], ACT.Tanh).then_inc(hi_made, 1)
                    act.activation(h_all[:, p, c, s, :], pre[c][:, :, 1], ACT.Tanh).then_inc(h_made, 1)

            def side_work(s, n, p, front, mid, back):
                q = 1 - p
                for i in range(2):
                    if mid and back and s == 0:
                        gelu_hi_piece(n + 1, 1, i)
                    if front and s in (1, 4):
                        copy_x(n + 2, p, s // 4, i)
                    if front and s in (2, 5):
                        copy_x_hi(n + 2, s // 5, i)
                    if mid and s in (7, 9):
                        z_hi_piece(n + 1, q, 1 - s // 9, i)
                    if back and s in (8, 11):
                        copy_y(n - 1, q, s // 11, i)
                    if front and s in (13, 15):
                        gelu_piece(n + 2, s // 15, i)
                    if front and s == 14:
                        gelu_hi_piece(n + 2, 0, i)

            act.wait_ge(s_zero, 1)
            for i in range(3):
                nc.scalar.dma_start(b_rows[32 * i:32 * i + 1, :],
                                    b.rearrange("(a d) -> a d", a=1)).then_inc(s_b, 16)
            nc.scalar.dma_start(biasT[:, :, :, :], bias2.rearrange("(q c p r) -> p q c r", q=4, c=C, p=P)
                                ).then_inc(s_bias2, 16)
            act.wait_ge(s_dve, VARIANCE)
            act.activation(stat[:, 3:4], stat[:, 2:3], ACT.Sqrt).then_inc(s_act, 1)
            for c in range(C):
                copy_x(0, 0, 0, c)
            for c in range(C):
                copy_x(0, 0, 1, c)
            act.wait_ge(s_prep_pe, 8)
            act.wait_ge(s_small, 16 * 4)
            for m in range(C):
                last = act.activation(hidT0[:, m, :], pre_gate[1][1][:, m * B:(m + 1) * B], ACT.Gelu,
                                      bias=cols[:, 2, m:m + 1])
            last.then_inc(s_hid0, 1)

            def copy_adapters(stage):
                act.wait_ge(s_wgen, 2 * stage + 1)
                act.activation(w_all[:, stage, 0:512], pre_gate[0][0][:, :], ACT.Copy).then_inc(s_wcopy, 1)

            for c in range(C):
                copy_x(1, 1, 0, c)
            copy_adapters(0)
            for c in range(C):
                copy_x(1, 1, 1, c)
            copy_adapters(1)
            for m in range(C):
                for half in range(2):
                    gelu_piece(0, m, half)
            act.wait_ge(s_rows_ps, 2)
            act.activation(a1T[:, :, :].rearrange("p g n -> p (g n)"), pre_gate[0][1][:, :],
                           ACT.Copy).then_inc(s_rows, 1)
            act.wait_ge(v_made, 1)
            act.wait_ge(mid_made, 4)
            for m in range(C):
                for half in range(2):
                    gelu_piece(1, m, half, pre_gate[1])
                    gelu_hi_piece(1, m, half, pre_gate[1])

            def body(n, p, i, front, mid, back):
                wait(act, y_made, 4 * (n - 1))
                for s in range(TB):
                    step(n, p, s)
                    side_work(s, n, p, front, mid, back)

            each_block(nc.scalar, body)
            for q in range(2):
                copy_y(NBLK - 1, (NBLK - 1) % 2, 0, q)

        @block.vector
        def _(dve):
            def mask_piece(n, made, masked, dst, bnk, j):
                if j == 0:
                    dve.wait_ge(made, n + 1)
                rows = slice(j * P // 2, (j + 1) * P // 2)
                dve.tensor_tensor(dst[rows, :, j, :], bnk[rows, 0:G * P].rearrange("p (g t) -> p g t", g=G),
                                  mask[rows, :, :].rearrange("p (o b) s -> p o (b s)", o=1)
                                  .broadcast_to([P // 2, G, P]), ALU.mult).then_inc(masked, 1)

            def add_y(n, p, g, c, s0=0, s1=TB):
                if g == 0 and c == 1:
                    dve.wait_ge(h_made, 2 * (TB * n + s1))
                    wait(dve, y_turned, 2 * (n - 1))
                bs = slice(g * BG, (g + 1) * BG)
                return dve.scalar_tensor_tensor(
                    yT[:, p, c, g * HALF:(g + 1) * HALF].rearrange("p (b s) -> p b s", b=BG)[:, :, s0:s1],
                    zp[:, p, c, s0:s1, bs, 1].rearrange("p s b -> p b s"), 2.0,
                    h_all[:, p, c, s0:s1, bs].rearrange("p s b -> p b s"), ALU.mult, ALU.add)

            def y_piece(n, p, g, c):
                add_y(n, p, g, c).then_inc(y_made, 1)

            def z_piece(n, p, m, g):
                if g == 0:
                    dve.wait_ge(mlp_made, 2 * n + 2 - m)
                    wait(dve, y_made, 4 * (n - 1) - 2 * m)
                c0 = g * HALF
                dve.scalar_tensor_tensor(
                    zp[:, p, m, :, g * BG:(g + 1) * BG, 1].rearrange("p s b -> p b s"),
                    mlp[m][:, c0:c0 + HALF].rearrange("p (b s) -> p b s", b=BG), 0.5,
                    xT[:, p, m, c0:c0 + HALF].rearrange("p (b s) -> p b s", b=BG),
                    ALU.mult, ALU.add).then_inc(z_made, 1)

            def lo_part(dst, full, hi, made):
                dve.tensor_tensor(dst, full, hi.bitcast(F32), ALU.subtract).then_inc(made, 1)

            def x_lo_piece(n, p, half, c):
                dve.wait_ge(x_hi_made, 4 * (n - 2) + 2 * half + c + 1)
                tokens = slice(half * HALF, (half + 1) * HALF)
                lo_part(x_lo[:, c, tokens], xT[:, p, c, tokens], x_hi[:, c, tokens], x_lo_made)

            def hid_lo_piece(n, m, half):
                dve.wait_ge(hid_hi_made, 4 * (n - 1) + 2 * m + half + 1)
                tokens = slice(half * HALF, (half + 1) * HALF)
                lo_part(hid_lo[:, m, tokens], hid[:, m, tokens], hid_hi[:, m, tokens], hid_lo_made)

            def z_lo_piece(n, p, m, g):
                dve.wait_ge(z_hi_made, 4 * (n - 1) + 2 * (1 - m) + g + 1)
                bs = slice(g * BG, (g + 1) * BG)
                lo_part(z_lo[:, m, :, bs], zp[:, p, m, :, bs, 1], z_hi[:, m, :, bs], z_lo_made)

            def leak_h(c, state, p, s):
                dve.scalar_tensor_tensor(gl[:, c, :, 1], state, leak_col[:, c:c + 1],
                                         zp[:, p, c, s, :, 1], ALU.mult, ALU.add).then_inc(leaked, 1)

            def step(n, p, s, front, mid, back):
                t = TB * n + s
                for c in range(C):
                    dve.wait_ge(gate_out, 2 * t + c + 1)
                    dve.wait_ge(leaked, 2 * t + c + 1)
                    dve.tensor_tensor_scan(pre[c][:, :, :].rearrange("p b j -> p (b j)"),
                                           zp[:, p, c, s, :, :].rearrange("p b j -> p (b j)"),
                                           gl[:, c, :, :].rearrange("p b j -> p (b j)"),
                                           0.0, ALU.mult, ALU.add).then_inc(pre_made, 1)
                side_work(s, n, p, front, mid, back)
                for c in range(C):
                    dve.wait_ge(h_made, 2 * t + c + 1)
                    dve.tensor_tensor(h_lo[:, c, :], h_all[:, p, c, s, :], h_hi[:, c, :],
                                      ALU.subtract).then_inc(lo_made, 1)
                if not (isinstance(n, int) and t == T - 1):
                    if s == TB - 1:
                        dve.wait_ge(z_made, 4 * (n + 2))
                    for c in range(C):
                        leak_h(c, h_all[:, p, c, s, :], *((p, s + 1) if s < TB - 1 else (1 - p, 0)))

            def side_work(s, n, p, front, mid, back):
                q = 1 - p
                if mid and back and s == 0:
                    hid_lo_piece(n + 1, 0, 1)
                if mid and s == 1:
                    hid_lo_piece(n + 1, 1, 0)
                if mid and s == 2:
                    mask_piece(n + 1, v_made, v_masked, v_sb, mlp[0], 0)
                if back and s in (3, 4):
                    y_piece(n - 1, q, 4 - s, 4 - s)
                if mid and s in (5, 6):
                    z_piece(n + 1, q, 1, s - 5)
                if mid and s == 7:
                    z_piece(n + 1, q, 0, 0)
                if front and s == 8:
                    x_lo_piece(n + 2, p, 1, 1)
                if mid and s == 10:
                    z_lo_piece(n + 1, q, 1, 0)
                if front and s == 9:
                    mask_piece(n + 2, u_made, u_masked, u_sb, mlp[1], 0)
                if mid and s in (11, 12):
                    z_lo_piece(n + 1, q, 0, s - 11)
                if front and s == 15:
                    hid_lo_piece(n + 2, 0, 0)

            def late_side_work(s, n, p, front, mid, back):
                q = 1 - p
                if not mid and s in (11, 12, 13, 14):
                    add_y(n, p, s % 2 ^ 1, (14 - s) // 2, 0, EARLY)
                if back and s == 0:
                    y_piece(n - 1, q, 0, 1)
                if mid and s == 1:
                    hid_lo_piece(n + 1, 1, 1)
                if mid and s == 2:
                    mask_piece(n + 1, v_made, v_masked, v_sb, mlp[0], 1)
                if front and s in (3, 4):
                    x_lo_piece(n + 2, p, 0, s - 3)
                if back and s == 5:
                    y_piece(n - 1, q, 1, 0)
                if front and s == 6:
                    x_lo_piece(n + 2, p, 1, 0)
                if mid and s == 7:
                    z_piece(n + 1, q, 0, 1)
                if mid and s == 10:
                    z_lo_piece(n + 1, q, 1, 1)
                if front and s == 9:
                    mask_piece(n + 2, u_made, u_masked, u_sb, mlp[1], 1)

            chain = [0]

            def link(ins):
                chain[0] += 1
                ins.then_inc(s_dve, 1)
                dve.wait_ge(s_dve, chain[0])

            dve.memset(b_rows[:, :], 0.0).then_inc(s_zero, 1)
            dve.wait_ge(s_x0, 16)
            link(dve.tensor_reduce(stat[:, 0:1], cond_sb[:, :], AX.X, ALU.add))
            link(dve.tensor_scalar(stat[:, 1:2], stat[:, 0:1], 1.0 / D, None, ALU.mult))
            link(dve.tensor_scalar(cond_n[:, :], cond_sb[:, :], stat[:, 1:2], None, ALU.subtract))
            link(dve.tensor_tensor(cond_sq[:, :], cond_n[:, :], cond_n[:, :], ALU.mult))
            link(dve.tensor_reduce(stat[:, 5:6], cond_sq[:, :], AX.X, ALU.add))
            link(dve.tensor_scalar(stat[:, 2:3], stat[:, 5:6], 1.0 / D, EPS, ALU.mult, ALU.add))
            dve.wait_ge(s_act, 1)
            link(dve.reciprocal(stat[:, 4:5], stat[:, 3:4]))
            dve.tensor_scalar(cond_n[:, :], cond_n[:, :], stat[:, 4:5], None, ALU.mult).then_inc(s_normed, 1)
            dve.wait_ge(s_prep_pe, 2)
            dve.tensor_copy(wT[:, 0:C, :].rearrange("p c n -> p (c n)"), pre_gate[0][0][:, :]).then_inc(s_prep_ev, 1)
            dve.tensor_scalar(wT[:, C:2 * C, :].rearrange("p c n -> p (c n)"), pre_gate[0][1][:, :], 2.0, None,
                              ALU.mult).then_inc(s_prep_ev, 1)
            dve.wait_ge(s_prep_pe, 3)
            dve.tensor_copy(upT[:, :, :].rearrange("p c n -> p (c n)"), spare[:, :]).then_inc(s_prep_ev, 1)
            dve.wait_ge(s_small, 16 * 4)
            dve.wait_ge(s_prep_pe, 7)
            dve.tensor_copy(condT[:, :, :].rearrange("p c b -> p (c b)"), pre_gate[1][0][:, 0:C * B])
            for c in range(C):
                last = dve.tensor_scalar(cT[:, c, :], pre_gate[1][0][:, (C + c) * B:(C + c + 1) * B],
                                         cols[:, 0, c:c + 1], cols[:, 1, c:c + 1], ALU.mult, ALU.add)
            last.then_inc(s_cond, 1)
            link(dve.memset(ones_bf[:, :], 1.0))
            link(dve.memset(u_sb[:, :, :, :].rearrange("p g j t -> p (g j t)"), 0.0))
            link(dve.memset(v_sb[:, :, :, :].rearrange("p g j t -> p (g j t)"), 0.0))
            link(dve.tensor_scalar(leak_col[:, :], cols[:, 3, :], -1.0, 1.0, ALU.mult, ALU.add))
            link(dve.tensor_copy(wh_part[:, 0, :, :], wT[:, 0:C, :]))
            link(dve.tensor_tensor(wh_rest[:, :, :], wT[:, 0:C, :], wh_part[:, 0, :, :], ALU.subtract))
            link(dve.tensor_copy(wh_part[:, 1, :, :], wh_rest[:, :, :]))
            link(dve.tensor_tensor(wh_part[:, 2, :, :], wh_rest[:, :, :], wh_part[:, 1, :, :], ALU.subtract))
            dve.wait_ge(s_b, 16 * 3)
            link(dve.memset(b_part[:, :], 0.0))
            link(dve.tensor_copy(b_hi[:, :], b_rows[:, :]))
            link(dve.tensor_tensor(b_rest[:, :], b_rows[:, :], b_hi[:, :], ALU.subtract))
            link(dve.tensor_copy(b_mid[:, :], b_rest[:, :]))
            link(dve.tensor_copy(b_part[0:1, :], b_hi[0:1, :]))
            link(dve.tensor_copy(b_part[32:33, :], b_mid[32:33, :]))
            link(dve.tensor_tensor(b_part[64:65, :], b_rest[64:65, :], b_mid[64:65, :], ALU.subtract))
            dve.wait_ge(s_base, 32)
            dve.wait_ge(s_prep_ev, 3)
            for hi, lo, full in ((down_hi, down_lo, down[:, :, :]), (up_hi, up_lo, upT[:, :, :]),
                                 (wz_hi, wz_lo, wT[:, C:2 * C, :])):
                link(dve.tensor_copy(hi[:, :, :], full))
                dve.tensor_tensor(lo[:, :, :], full, hi[:, :, :].bitcast(F32), ALU.subtract).then_inc(s_parts, 1)
            def copy_adapters(stage):
                dve.wait_ge(s_wgen, 2 * stage + 2)
                dve.tensor_copy(w_all[:, stage, 512:1024], pre_gate[0][1][:, :]).then_inc(s_wcopy, 1)

            def add_bias2(stage, banks):
                q0 = 2 - 2 * stage
                for rh in range(2):
                    dve.wait_ge(s_wturn, 2 * stage + rh + 1)
                    r0 = 4 * rh
                    dve.tensor_tensor(
                        adapt[:, q0:q0 + 2, :, :, r0:r0 + 4].rearrange("p q c b r -> p (q c) b r"),
                        banks[rh][:, :].rearrange("p (r e b) -> p e b r", r=4, b=B),
                        biasT[:, q0:q0 + 2, :, r0:r0 + 4].rearrange("p q c (o r) -> p (q c) o r", o=1)
                        .broadcast_to([P, 2 * C, B, 4]), ALU.add).then_inc(s_adapt, 1)

            copy_adapters(0)
            dve.wait_ge(s_bias2, 16)
            add_bias2(0, (turn, spare))
            dve.wait_ge(s_rows_ps, 1)
            dve.tensor_copy(b2T[:, :, :].rearrange("p g n -> p (g n)"), pre_gate[0][1][:, :]).then_inc(s_rows, 1)
            dve.wait_ge(s_mask, 5)
            for n in range(2):
                for j in range(2):
                    mask_piece(n, u_made, u_masked, u_sb, spare, j)
            copy_adapters(1)
            add_bias2(1, (turn, spare))
            for j in range(2):
                mask_piece(0, v_made, v_masked, v_sb, spare, j)
            for m in (1, 0):
                for g in range(G):
                    z_piece(0, 0, m, g)
            for half in range(2):
                hid_lo_piece(1, 0, half)
            dve.wait_ge(s_pairs, 1)
            dve.wait_ge(z_made, 4)
            for c in range(C):
                leak_h(c, condT[:, c, :], 0, 0)

            def body(n, p, i, front, mid, back):
                for s in range(TB):
                    step(n, p, s, front, mid, back)
                    late_side_work(s, n, p, front, mid, back)

            each_block(nc.vector, body)
            last, p = NBLK - 1, (NBLK - 1) % 2
            for c in (1, 0):
                for g in range(G):
                    add_y(last, p, g, c, EARLY, TB).then_inc(y_made, 1)
            dve.wait_ge(y_stored[p], 8 * TILES * (last - p))
            dve.wait_ge(y_turned, 2 * NBLK)
            for q in range(2):
                dve.tensor_copy(y_nat[:, p, 2 + q, :], mlp[0][:, q * D:(q + 1) * D]).then_inc(last_copied, 1)


_INS = ["x", "cond_1024", "L0_cond_base_up", "L0_cond_base_down", "L0_cond_ln_gamma", "L0_cond_ln_beta",
        "L0_cond_W1", "L0_cond_bias1", "L0_cond_W2", "L0_cond_bias2", "L1_cond_W", "L1_cond_b",
        "L1_cond_alpha"]


def kernel(**inputs):
    import numpy as np
    import concourse.bacc as bacc
    from concourse.bass_utils import run_bass_kernel_spmd

    nc = bacc.Bacc("TRN2", target_bir_lowering=False, num_devices=1)
    arrays, args = {}, []
    for name in _INS:
        a = np.ascontiguousarray(inputs[name])
        arrays[f"in_{name}"] = a
        args.append(nc.dram_tensor(f"in_{name}", a.shape, mybir.dt.from_np(a.dtype), kind="ExternalInput").ap())
    shape = inputs["x"].shape
    args.append(nc.dram_tensor("out_0", shape, F32, kind="ExternalOutput").ap())
    build(nc, *args)
    r = run_bass_kernel_spmd(nc, [arrays], core_ids=[0])
    return r.results[0]["out_0"]
```
